# Optimizing a Trainium2 kernel written in Bass

```python
import numpy as np
import jax
import jax.numpy as jnp

def _softmax(x, axis=-1):
    return jax.nn.softmax(x, axis=axis)

def _gelu(x):
    return jax.nn.gelu(x, approximate=True)

def _silu(x):
    return jax.nn.silu(x)

def _sigmoid(x):
    return jax.nn.sigmoid(x)

def _layernorm(x, axis=-1, eps=1e-05):
    m = jnp.mean(x, axis=axis, keepdims=True)
    v = jnp.var(x, axis=axis, keepdims=True)
    return (x - m) / jnp.sqrt(v + eps)

def _scatter_add(tgt, idx, src, axis=0):
    return tgt.at[idx].add(src)

def _segment_sum(src, seg, n):
    return jax.ops.segment_sum(src, seg, n)
kernel_name = 'mk_flamingo_gated_d1_seqx_r8_2df15f'

def setup_inputs(seed: int=0):
    np.random.seed(seed)
    _w = jnp.asarray

    def _rec_inputs():
        import jax
        import jax.numpy as jnp
        _rk = jax.random.key(seed)
        x = -0.000125 + 0.9999 * jax.random.normal(jax.random.fold_in(_rk, 1), (8, 128, 512), jnp.float32)
        _lenS = 128 - jax.random.randint(jax.random.fold_in(_rk, 7), (8,), 0, max(1, 128 // 4) + 1, jnp.int32)
        _lenS2 = 128 - jax.random.randint(jax.random.fold_in(_rk, 8), (8,), 0, max(1, 128 // 4) + 1, jnp.int32)
        _ctx_4096P = jax.random.normal(jax.random.fold_in(_rk, 11), (8, 16, 512), jnp.float32)
        _ctx_4096c = jax.random.dirichlet(jax.random.fold_in(_rk, 511), 0.3 * jnp.ones((16,), jnp.float32), (8, 128))
        _ctx_4096t = jnp.einsum('bsk,bkd->bsd', _ctx_4096c, _ctx_4096P)
        _ctx_4096t = _ctx_4096t * jax.lax.rsqrt(jnp.mean(jnp.square(_ctx_4096t)) + 1e-12) * 0.953939
        ctx_4096 = -1.52775e-05 + 0.999936 * (_ctx_4096t + 0.3 * jax.random.normal(jax.random.fold_in(_rk, 611), (8, 128, 512), jnp.float32))
        _validS = jnp.arange(128)[None, :] < _lenS[:, None]
        _validS2 = jnp.arange(128)[None, :] < _lenS2[:, None]
        _causal = jnp.tril(jnp.ones((128, 128), dtype=bool))
        mask_Bx1x4096_ff1 = jnp.where(jnp.ones((8, 1, 512), dtype=bool), 1.0, 0.0).astype(jnp.float32)
        _g = jax.random.normal(jax.random.fold_in(_rk, 9001), (2, 1), jnp.float32)
        _g = jnp.sign(_g) * jnp.maximum(jnp.abs(_g), 1.0) + (_g == 0) * 1.0
        g_xattn = _g[0]
        g_ffn = _g[1]
        return (x, ctx_4096, mask_Bx1x4096_ff1, g_xattn, g_ffn)
    x, ctx_4096, mask_Bx1x4096_ff1, g_xattn, g_ffn = _rec_inputs()

    def _L0_xattn_setup():
        import jax, jax.numpy as jnp
        import numpy as np
        W = 128
        H = 8
        D = 128
        DK = D // 2

        def _to_patches(x):
            b, d, s = x.shape
            np_ = s // W
            return x.reshape(b, d, np_, W).transpose(0, 2, 1, 3).reshape(b * np_, d, W)
        key = jax.random.key(seed)
        ks = jax.random.split(key, 10)
        B, S = (8, 512)
        qk = jax.random.normal(ks[0], (B, D, S), dtype=jnp.float32)
        v = jax.random.normal(ks[1], (B, D, S), dtype=jnp.float32)
        masks = jnp.ones((B, 1, S), dtype=jnp.float32)
        sc = 1.0 / np.sqrt(D)
        Wq = jax.random.normal(ks[2], (DK, D), dtype=jnp.float32) * sc
        bq = jnp.zeros((DK,), dtype=jnp.float32)
        Wk = jax.random.normal(ks[3], (DK, D), dtype=jnp.float32) * sc
        bk = jnp.zeros((DK,), dtype=jnp.float32)
        Wv = jax.random.normal(ks[4], (DK, D), dtype=jnp.float32) * sc
        bv = jnp.zeros((DK,), dtype=jnp.float32)
        Wo = jax.random.normal(ks[5], (D, DK), dtype=jnp.float32) * (1.0 / np.sqrt(DK))
        bo = jnp.zeros((D,), dtype=jnp.float32)
        return dict(qk=qk, v=v, masks=masks, Wq=Wq, bq=bq, Wk=Wk, bk=bk, Wv=Wv, bv=bv, Wo=Wo, bo=bo)
    _L0_xattn_all = _L0_xattn_setup()
    _L0_xattn_in = {k: v for k, v in _L0_xattn_all.items() if k in ('Wq', 'bq', 'Wk', 'bk', 'Wv', 'bv', 'Wo', 'bo')}
    del _L0_xattn_all

    def _L0_ffn_setup():
        import jax, jax.numpy as jnp
        import numpy as np
        TOP_K = 2
        key = jax.random.key(seed)
        k0, k1, k2 = jax.random.split(key, 3)
        B, S, D, H, E = (4, 256, 512, 512, 8)
        sc = 1.0 / np.sqrt(D).astype(np.float32)
        x = jax.random.normal(k0, (B, S, D), dtype=jnp.float32)
        W_gate = jax.random.normal(k1, (D, E), dtype=jnp.float32) * sc
        b_gate = jnp.zeros((E,), dtype=jnp.float32)
        W_e = jax.random.normal(k2, (E, D, H), dtype=jnp.float32) * sc
        b_e = jnp.zeros((E, H), dtype=jnp.float32)
        return {'x': x, 'W_gate': W_gate, 'b_gate': b_gate, 'W_e': W_e, 'b_e': b_e}
    _L0_ffn_all = _L0_ffn_setup()
    _L0_ffn_in = {k: v for k, v in _L0_ffn_all.items() if k in ('W_gate', 'b_gate', 'W_e', 'b_e')}
    del _L0_ffn_all
    return {'x': x, 'ctx_4096': ctx_4096, 'mask_Bx1x4096_ff1': mask_Bx1x4096_ff1, 'g_xattn': g_xattn, 'g_ffn': g_ffn, 'L0_xattn_Wq': _L0_xattn_in['Wq'], 'L0_xattn_bq': _L0_xattn_in['bq'], 'L0_xattn_Wk': _L0_xattn_in['Wk'], 'L0_xattn_bk': _L0_xattn_in['bk'], 'L0_xattn_Wv': _L0_xattn_in['Wv'], 'L0_xattn_bv': _L0_xattn_in['bv'], 'L0_xattn_Wo': _L0_xattn_in['Wo'], 'L0_xattn_bo': _L0_xattn_in['bo'], 'L0_ffn_W_gate': _L0_ffn_in['W_gate'], 'L0_ffn_b_gate': _L0_ffn_in['b_gate'], 'L0_ffn_W_e': _L0_ffn_in['W_e'], 'L0_ffn_b_e': _L0_ffn_in['b_e']}

def reference(x, ctx_4096, mask_Bx1x4096_ff1, g_xattn, g_ffn, L0_xattn_Wq, L0_xattn_bq, L0_xattn_Wk, L0_xattn_bk, L0_xattn_Wv, L0_xattn_bv, L0_xattn_Wo, L0_xattn_bo, L0_ffn_W_gate, L0_ffn_b_gate, L0_ffn_W_e, L0_ffn_b_e):
    import jax
    import jax.numpy as jnp

    def _L0_xattn_ref(qk, v, masks, Wq, bq, Wk, bk, Wv, bv, Wo, bo):
        import jax, jax.numpy as jnp
        import numpy as np
        W = 128
        H = 8
        D = 128
        DK = D // 2

        def _to_patches(x):
            b, d, s = x.shape
            np_ = s // W
            return x.reshape(b, d, np_, W).transpose(0, 2, 1, 3).reshape(b * np_, d, W)
        B, _, S = qk.shape
        np_ = S // W
        qp = _to_patches(qk)
        vp = _to_patches(v)
        mp = _to_patches(masks)
        q = jnp.einsum('ed,bdw->bew', Wq, qp) + bq[:, None]
        k = jnp.einsum('ed,bdw->bew', Wk, qp) + bk[:, None]
        val = jnp.einsum('ed,bdw->bew', Wv, vp) + bv[:, None]
        BN = q.shape[0]
        dh = DK // H
        qh = q.reshape(BN, H, dh, W)
        kh = k.reshape(BN, H, dh, W)
        vh = val.reshape(BN, H, dh, W)
        scores = jnp.einsum('bhdi,bhdj->bhij', qh, kh) / jnp.sqrt(jnp.asarray(dh, qh.dtype))
        scores = jnp.where(mp[:, :, None, :] > 0, scores, jnp.asarray(-1000000000.0, scores.dtype))
        attn = jax.nn.softmax(scores, axis=-1)
        o = jnp.einsum('bhij,bhdj->bhdi', attn, vh).reshape(BN, DK, W)
        o = jax.nn.gelu(o, approximate=False)
        out = jnp.einsum('de,bew->bdw', Wo, o) + bo[:, None]
        out = out.reshape(B, np_, D, W).transpose(0, 2, 1, 3).reshape(B, D, S)
        out = out * masks
        return out

    def _L0_ffn_ref(x, W_gate, b_gate, W_e, b_e):
        import jax, jax.numpy as jnp
        import numpy as np
        TOP_K = 2
        logits = x @ W_gate + b_gate
        _, top_idx = jax.lax.top_k(logits, TOP_K)
        y_all = jax.nn.relu(jnp.einsum('bsd,edh->bseh', x, W_e) + b_e)
        y = jnp.take_along_axis(y_all, top_idx[..., None], axis=2)
        return y.mean(axis=2)
    x = x + jnp.tanh(g_xattn[0]) * _L0_xattn_ref(_layernorm(x, axis=-1), ctx_4096, mask_Bx1x4096_ff1, L0_xattn_Wq, L0_xattn_bq, L0_xattn_Wk, L0_xattn_bk, L0_xattn_Wv, L0_xattn_bv, L0_xattn_Wo, L0_xattn_bo)
    x = x + jnp.tanh(g_ffn[0]) * _L0_ffn_ref(_layernorm(x, axis=-1), L0_ffn_W_gate, L0_ffn_b_gate, L0_ffn_W_e, L0_ffn_b_e)
    return x

_drawn_inputs = setup_inputs


def setup_inputs(seed=0):
    import zlib

    import numpy as np

    out = dict(_drawn_inputs(seed))
    spreads = {'L0_xattn_bq': (0.0, 0.282),
     'L0_xattn_bk': (0.0, 0.8),
     'L0_xattn_bv': (0.0, 0.1),
     'L0_xattn_bo': (0.0, 0.1),
     'L0_ffn_b_gate': (0.0, 0.1),
     'L0_ffn_b_e': (0.0, 0.1)}
    factors = {}
    for name, (base, spread) in spreads.items():
        noise = np.random.default_rng([zlib.crc32(name.encode()), seed]).standard_normal(out[name].shape)
        drawn = base * np.exp(spread * noise) if base else spread * noise
        out[name] = jnp.asarray(drawn.astype(out[name].dtype))
    for name, factor in factors.items():
        out[name] = (out[name] * factor).astype(out[name].dtype)
    return out
```

```python
from contextlib import ExitStack

import concourse.bass as bass
from concourse import mybir

F32 = mybir.dt.float32
F16 = mybir.dt.float16
BF16 = mybir.dt.bfloat16
I32 = mybir.dt.int32
ALU = mybir.AluOpType
ACT = mybir.ActivationFunctionType
AX = mybir.AxisListType

START = 1
MAXIMUM = bass.bass_isa.ReduceOp.max

P = 128
B, D, S = 8, 128, 512
W = 128
NWIN = S // W
H, DH = 8, 8
DK = H * DH
NG = 2
HG = H // NG
QUAD = HG * DH
E = 8
KC = S // P
EPS = 1e-5
NORM_BOUND = 22.7
QK_FLOOR = 8.0
QK_TOP = 2.0 ** 11
WE_TOP = 2.0 ** 10
AUX = 3 * QUAD
ROWS_MASK = AUX + 1
ROWS_ALL = AUX + 1 + 2 * HG
MASK_Q = 2.0 ** 15
AUX_K = 2.0 ** 14
THIRDS = 3
VC = DH + 1
STACK_DMAS = 12

C_IDENT = 0
C_HEAD = C_IDENT + P
C_ONE = C_HEAD + HG
C_EARLIER = C_ONE + HG
C_SIDE = C_EARLIER + E * E
C_END = C_SIDE + 2


def shape_constants():
    import numpy as np

    c = np.zeros((P, C_END), np.float32)
    c[:, C_IDENT:C_IDENT + P] = np.eye(P)
    for h in range(HG):
        for third in range(3):
            at = third * QUAD + h * DH
            c[at:at + DH, C_HEAD + h] = 1
        c[AUX, C_HEAD + h] = 1
        c[AUX + 1 + h, C_ONE + h] = AUX_K
        c[AUX + 1 + HG + h, C_ONE + h] = AUX_K
    for e in range(E):
        for j in range(e):
            c[:, C_EARLIER + e * E + j] = 1
    c[0:DK, C_SIDE] = 1
    c[DK:2 * DK, C_SIDE + 1] = 1
    return c


def build(nc, x, ctx_in, mask, g_xattn, g_ffn, wq, bq, wk, bk, wv, bv, wo, bo,
          w_gate, b_gate, w_e, b_e, consts, out):
    stack = ExitStack()
    with stack:
        def sb(name, shape, dt=F32):
            return stack.enter_context(nc.sbuf_tensor(name, shape, dt))

        def pb(name, shape, dt=F32):
            return stack.enter_context(nc.psum_tensor(name, shape, dt))

        def sem(name):
            return stack.enter_context(nc.semaphore(name))

        x_all = sb("x_all", [P, B, S])
        mask_all = sb("mask_all", [P, B, S])
        expert_bias = sb("expert_bias", [P, E, S])
        we_in = sb("we_in", [P, 2, KC, S])
        we_hi = sb("we_hi", [P, E, KC, S], F16)
        we_lo = sb("we_lo", [P, E, KC, S], F16)
        ctx_sb = sb("ctx_sb", [P, 2, S])
        const = sb("const", [P, C_END])
        w_rows = sb("w_rows", [P, 4, P])
        wqk_t = sb("wqk_t", [P, P])
        wv_t = sb("wv_t", [P, DK])
        wo_t = sb("wo_t", [DK, P])
        bv_b = sb("bv_b", [P, DK])
        wg_in = sb("wg_in", [P, KC, E])
        wg_rest = sb("wg_rest", [P, KC, E])
        wg_thirds = sb("wg_thirds", [P, KC, THIRDS, E], BF16)
        ident16 = sb("ident16", [P, P], F16)
        col = sb("col", [P, 16])
        bqk, bo_c, g2, tg, scale_qk = col[:, 0:1], col[:, 1:2], col[:, 2:4], col[:, 4:6], col[:, 6:7]
        bias_qk, exp_scale, bound, zero_c = col[:, 7:8], col[:, 8:9], col[:, 9:10], col[:, 10:11]
        half_neg = sb("half_neg", [P, 1])
        bg_b = sb("bg_b", [P, E])
        qk_small = sb("qk_small", [P, 8])
        we_amax = sb("we_amax", [P, E])
        we_amax_all = sb("we_amax_all", [P, E])
        we_pow = sb("we_pow", [P, E])
        we_scale = sb("we_scale", [P, E])
        we_unscale = sb("we_unscale", [P, E])

        stats1 = sb("stats1", [P, B, 6])
        mean_var1 = sb("mean_var1", [P, B, 2])
        rstd1 = sb("rstd1", [P, B, 2])
        xn = sb("xn", [P, S])
        qk32 = sb("qk32", [P, S])
        qk_hi = sb("qk_hi", [P, S], F16)
        qk_lo = sb("qk_lo", [P, S], F16)
        q_stack = sb("q_stack", [P, 2, NG, S], F16)
        k_rows = sb("k_rows", [P, NG, S], F16)
        k_stack = sb("k_stack", [P, 2, NG, HG, S], F16)
        row_max = sb("row_max", [P, NG, NWIN, HG])
        shifts = sb("shifts", [P, NG * NWIN, 1 + 2 * HG], F16)
        prob32 = sb("prob32", [P, 2, H * W])
        prob_hi = sb("prob_hi", [P, 2, H * W], F16)
        prob_lo = sb("prob_lo", [P, 2, H * W], F16)
        v32 = sb("v32", [P, NWIN * H, DH])
        v_thirds = sb("v_thirds", [P, 2, NWIN * H, THIRDS, VC], BF16)
        o_sum = sb("o_sum", [P, NWIN * H, VC])
        o_den = sb("o_den", [P, NWIN * H])
        o_norm = sb("o_norm", [P, NWIN * H, DH])
        o_gelu = sb("o_gelu", [DK, S])
        attn_out = sb("attn_out", [P, S])

        stats2 = sb("stats2", [P, 6])
        mean_var2 = sb("mean_var2", [P, 4])
        xn2 = sb("xn2", [P, S])
        xt_hi = sb("xt_hi", [P, 2, KC, P], F16)
        xt_lo = sb("xt_lo", [P, 2, KC, P], F16)
        logit = sb("logit", [P, 2, E])
        pairs = sb("pairs", [P, 2, E, E])
        rank = sb("rank", [P, 2, E])
        gate = sb("gate", [P, 2, E])
        expert_out = sb("expert_out", [P, 2, S])
        total = sb("total", [P, 2, S])

        score = [pb(f"score{i}", [P, H * W]) for i in range(2)]
        ffn_bank = [pb(f"ffn{i}", [P, S]) for i in range(2)]
        pv = pb("pv", [P, S])
        misc = pb("misc", [P, S])
        pv16 = pv[:, :].bitcast(F16)

        const_in, wqk_in, x0_in, xrest_in, mask_in = map(sem, ("const_in", "wqk_in", "x0_in", "xrest_in", "mask_in"))
        wvo_in, small_in, bias_in = map(sem, ("wvo_in", "small_in", "bias_in"))
        ctx_loaded = [sem(f"ctx_loaded{i}") for i in range(2)]
        we_loaded = [sem(f"we_loaded{i}") for i in range(2)]
        s_ident, s_wt, s_wt_copied, s_sums, s_bound, s_scale, s_tanh = map(
            sem, ("s_ident", "s_wt", "s_wt_copied", "s_sums", "s_bound", "s_scale", "s_tanh"))
        s_wot, s_wg, s_init, s_amax, s_amax_all, s_wscale, s_wlo, s_whi, s_ebias = map(
            sem, ("s_wot", "s_wg", "s_init", "s_amax", "s_amax_all", "s_wscale", "s_wlo", "s_whi", "s_ebias"))
        s_stat, s_var1, s_rstd1 = map(sem, ("s_stat", "s_var1", "s_rstd1"))
        xn_ready, qk_proj, qk_scaled, k_masked, hi_ready, lo_ready, stacks_in = map(
            sem, ("xn_ready", "qk_proj", "qk_scaled", "k_masked", "hi_ready", "lo_ready", "stacks_in"))
        mask_row, k_ready, v_proj, v_biased, v_step, v_ready = map(
            sem, ("mask_row", "k_ready", "v_proj", "v_biased", "v_step", "v_ready"))
        scores, max_done, max_hi, shifts_ready, shifts_t, shift_rows = map(
            sem, ("scores", "max_done", "max_hi", "shifts_ready", "shifts_t", "shift_rows"))
        scores_t, exp_done, hi_done, lo_done, pv_done = map(
            sem, ("scores_t", "exp_done", "hi_done", "lo_done", "pv_done"))
        pv_read, den_ready, o_ready, o_t, gelu_done, wo_done, attn_masked, x1_ready = map(
            sem, ("pv_read", "den_ready", "o_ready", "o_t", "gelu_done", "wo_done", "attn_masked", "x1_ready"))
        s_stat2, s_var2, s_rstd2, xn2_ready, xn2_t, xt_hi_ready, xt_lo_ready = map(
            sem, ("s_stat2", "s_var2", "s_rstd2", "xn2_ready", "xn2_t", "xt_hi_ready", "xt_lo_ready"))
        logits, logits_read, s_gate, gates_ready = map(sem, ("logits", "logits_read", "s_gate", "gates_ready"))
        ffn_done, biased, relu_done, summed, out_ready = map(
            sem, ("ffn_done", "biased", "relu_done", "summed", "out_ready"))
        out_done = [sem(f"out_done{i}") for i in range(2)]

        block = stack.enter_context(nc.Block())

        def wait(eng, semaphore, value):
            if isinstance(value, int) and value <= 0:
                return
            eng.wait_ge(semaphore, value)

        def wait_alone(eng, *waits):
            for _, value in waits:
                if not isinstance(value, int):
                    eng.lower_val(value)
            eng.wait_ge(const_in, 16)
            for semaphore, value in waits:
                wait(eng, semaphore, value)

        def steps(eng, step):
            step(-1, 1, ffn=False, attn=False, prep=True)
            step(0, 0, ffn=False, attn=True, prep=True)
            with eng.Fori(0, (B - 2) // 2) as i:
                step(2 * i + 1, 1, ffn=True, attn=True, prep=True)
                step(2 * i + 2, 0, ffn=True, attn=True, prep=True)
            step(B - 1, 1, ffn=True, attn=True, prep=False)
            step(B, 0, ffn=True, attn=False, prep=False)

        @block.sync
        def _(sp):
            for half in out_done:
                sp.sem_inc(half, 16 * START)
            sp.dma_start(w_rows[0:DK, 0, :], wq).then_inc(wqk_in, 16)
            sp.dma_start(w_rows[DK:2 * DK, 0, :], wk).then_inc(wqk_in, 16)
            sp.dma_start(const[:, :], consts).then_inc(const_in, 16)
            sp.dma_start(x_all[:, 0, :], x[0]).then_inc(x0_in, 16)
            sp.dma_start(bqk[0:DK, :], bq.rearrange("(e o) -> e o", o=1)).then_inc(small_in, 16)
            sp.dma_start(bqk[DK:2 * DK, :], bk.rearrange("(e o) -> e o", o=1)).then_inc(small_in, 16)
            sp.dma_start(bo_c, bo.rearrange("(e o) -> e o", o=1)).then_inc(small_in, 16)
            sp.dma_start(g2[:, 0:1], g_xattn.rearrange("(o e) -> o e", o=1).broadcast_to([P, 1])).then_inc(small_in, 16)
            sp.dma_start(g2[:, 1:2], g_ffn.rearrange("(o e) -> o e", o=1).broadcast_to([P, 1])).then_inc(small_in, 16)
            sp.dma_start(bv_b[:, :], bv.rearrange("(o e) -> o e", o=1).broadcast_to([P, DK])).then_inc(small_in, 16)
            sp.dma_start(bg_b[:, :], b_gate.rearrange("(o e) -> o e", o=1).broadcast_to([P, E])).then_inc(small_in, 16)
            sp.dma_start(wg_in[:, :, :], w_gate.rearrange("(k p) e -> p k e", p=P)).then_inc(small_in, 16)
            sp.dma_start(w_rows[0:DK, 1, :], wv).then_inc(wvo_in, 16)
            sp.dma_start(w_rows[:, 2, 0:DK], wo).then_inc(wvo_in, 16)
            sp.dma_start(ctx_sb[:, 0, :], ctx_in[0]).then_inc(ctx_loaded[0], 16)
            sp.dma_start(mask_all[:, :, :], mask.rearrange("b o s -> o b s").broadcast_to([P, B, S])).then_inc(mask_in, 16)
            for b in range(1, B):
                sp.dma_start(x_all[:, b, :], x[b]).then_inc(xrest_in, 16)
            sp.dma_start(expert_bias[:, :, :],
                         b_e.rearrange("(o e) s -> o e s", o=1).broadcast_to([P, E, S])).then_inc(bias_in, 16)

            def step(t, par, ffn, attn, prep):
                if prep:
                    n, np_ = t + 1, (par + 1) % 2
                    if not (isinstance(n, int) and n == 0):
                        wait_alone(sp, (v_proj, n - 1))
                        sp.dma_start(ctx_sb[:, np_, :], ctx_in[n]).then_inc(ctx_loaded[np_], 16)
                    wait_alone(sp, (hi_ready, n + 1), (lo_ready, n + 1), (scores_t, NWIN * (n - 1)), (k_ready, n))
                    for g in range(NG):
                        q_at, k_at = QUAD * g, DK + QUAD * g
                        halves = (qk_hi, qk_lo, qk_hi)
                        for third in range(3):
                            sp.dma_start(k_rows[QUAD * third:QUAD * (third + 1), g, :],
                                         (qk_hi, qk_hi, qk_lo)[third][k_at:k_at + QUAD, :]).then_inc(stacks_in, 16)
                            sp.dma_start(q_stack[QUAD * third:QUAD * (third + 1), np_, g, :],
                                         halves[third][q_at:q_at + QUAD, :]).then_inc(stacks_in, 16)
                if ffn:
                    f, fpar = t - 1, (par + 1) % 2
                    wait_alone(sp, (out_ready, f + 1))
                    sp.dma_start(out[f], total[:, fpar, :]).then_inc(out_done[fpar], 16)

            steps(sp, step)
            for half in out_done:
                sp.wait_ge(half, 16 * START + 16 * B // 2)

        @block.tensor
        def _(pe):
            pe.sem_inc(ffn_done, START)
            pe.wait_ge(const_in, 16)
            pe.wait_ge(wqk_in, 32)
            ident32 = const[:, C_IDENT:C_IDENT + P]
            pe.transpose(misc[:, 0:P], w_rows[:, 0, :], ident32).then_inc(s_wt, 1)
            pe.wait_ge(wvo_in, 32)
            pe.transpose(pv[:, 0:DK], w_rows[0:DK, 1, :], ident32[0:DK, 0:DK]).then_inc(s_wt, 1)
            pe.transpose(ffn_bank[0][0:DK, 0:P], w_rows[:, 2, 0:DK], ident32).then_inc(s_wt, 1)
            pe.wait_ge(s_wt_copied, 3)

            def score_maxima(n, np_, w):
                slot = score[w % 2]
                if w < 2:
                    wait(pe, exp_done, NWIN * (n - 1) + w + 3)
                else:
                    wait(pe, max_done, NWIN * n + w - 1)
                if w == 0:
                    pe.wait_ge(stacks_in, 16 * STACK_DMAS * (n + 1))
                    pe.wait_ge(k_ready, n + 1)
                for g in range(NG):
                    mm = pe.matmul(slot[:, g * HG * W:(g + 1) * HG * W].rearrange("p (h j) -> p h j", h=HG),
                                   q_stack[0:ROWS_MASK, np_, g, w * W:(w + 1) * W],
                                   k_stack[0:ROWS_MASK, np_, g, :, w * W:(w + 1) * W], start=True, stop=True)
                mm.then_inc(scores, 1)

            def score_shifted(t, par, w):
                slot = score[w % 2]
                if w < 2:
                    wait(pe, max_done, NWIN * t + w + 3)
                else:
                    wait(pe, exp_done, NWIN * t + w - 1)
                if w == 0:
                    pe.wait_ge(shift_rows, t + 1)
                for h in range(H):
                    g, hg = h // HG, h % HG
                    mm = pe.matmul(slot[:, h * W:(h + 1) * W],
                                   k_stack[0:ROWS_ALL, par, g, hg, w * W:(w + 1) * W],
                                   q_stack[0:ROWS_ALL, par, g, w * W:(w + 1) * W], start=True, stop=True)
                mm.then_inc(scores_t, 1)

            def weigh_values(t, par, w):
                pe.wait_ge(lo_done, NWIN * t + w + 1)
                if w == 0:
                    pe.wait_ge(v_ready, t + 1)
                if w % 2 == 0:
                    wait(pe, pv_read, 2 * t + w // 2)
                for h in range(H):
                    at = ((w % 2) * H + h) * THIRDS * VC
                    v = v_thirds[:, par, w * H + h, :, :].rearrange("p q c -> p (q c)")
                    for part, half in enumerate((prob_hi, prob_lo)):
                        mm = pe.matmul(pv[:, at:at + THIRDS * VC], half[:, w % 2, h * W:(h + 1) * W], v,
                                       start=(part == 0), stop=(part == 1))
                mm.then_inc(pv_done, 1)

            def expert(f, fpar, e, first):
                if e == 0:
                    pe.wait_ge(xt_hi_ready, f + 1)
                    pe.wait_ge(xt_lo_ready, f + 1)
                if first:
                    pe.wait_ge(s_wlo, e + 1)
                pe.wait_ge(relu_done, START + E * f + max(e - 1, 0))
                for c in range(KC):
                    for i, (xs, ws) in enumerate(((xt_hi, we_hi), (xt_hi, we_lo), (xt_lo, we_hi))):
                        mm = pe.matmul(ffn_bank[e % 2][:, :], xs[:, fpar, c, :], ws[:, e, c, :],
                                       start=(c == 0 and i == 0), stop=(c == KC - 1 and i == 2))
                mm.then_inc(ffn_done, 1)

            def step(t, par, ffn, attn, prep):
                n, npar = t + 1, (par + 1) % 2
                f, fpar = t - 1, (par + 1) % 2
                first = not isinstance(t, int) or t < 3

                def ex(e):
                    if ffn:
                        expert(f, fpar, e, first)

                if attn:
                    score_shifted(t, par, 0)
                if prep:
                    pe.wait_ge(xn_ready, n + 1)
                    wait(pe, v_biased, n)
                    wait(pe, logits_read, t)
                    pe.matmul(misc[:, :], wqk_t[:, :], xn[:, :], start=True, stop=True).then_inc(qk_proj, 1)
                if attn:
                    score_shifted(t, par, 1)
                ex(0)
                if prep:
                    pe.wait_ge(qk_scaled, n + 1)
                    if isinstance(t, int):
                        pe.wait_ge(ctx_loaded[npar], 16 * (n // 2 + 1))
                    else:
                        pe.wait_ge(ctx_loaded[npar], (n - npar) * 8 + 16)
                    for w in range(NWIN):
                        mm = pe.matmul(misc[:, w * DK:(w + 1) * DK], ctx_sb[:, npar, w * W:(w + 1) * W],
                                       wv_t[:, :], start=True, stop=True)
                    mm.then_inc(v_proj, 1)
                if attn:
                    weigh_values(t, par, 0)
                    score_shifted(t, par, 2)
                ex(1)
                if attn:
                    weigh_values(t, par, 1)
                    score_shifted(t, par, 3)
                ex(2)
                if attn:
                    weigh_values(t, par, 2)
                ex(3)
                if attn:
                    weigh_values(t, par, 3)
                if prep:
                    score_maxima(n, npar, 0)
                ex(4)
                if prep:
                    score_maxima(n, npar, 1)
                if attn:
                    wait_alone(pe, (o_ready, t + 1))
                    if prep:
                        pe.wait_ge(v_biased, n + 1)
                    wait(pe, logits_read, t)
                    for w in range(NWIN):
                        mm = pe.transpose(misc[0:DK, w * W:(w + 1) * W],
                                          o_norm[:, w * H:(w + 1) * H, :].rearrange("p h d -> p (h d)"),
                                          const[:, C_IDENT:C_IDENT + P])
                    mm.then_inc(o_t, 1)
                ex(5)
                if prep:
                    score_maxima(n, npar, 2)
                if attn:
                    pe.wait_ge(gelu_done, t + 1)
                    pe.matmul(misc[:, :], wo_t[:, :], o_gelu[:, :], start=True, stop=True).then_inc(wo_done, 1)
                ex(6)
                if prep:
                    score_maxima(n, npar, 3)
                ex(7)
                if attn:
                    pe.wait_ge(xn2_ready, t + 1)
                    for c in range(KC):
                        mm = pe.transpose(misc[:, c * P:(c + 1) * P], xn2[:, c * P:(c + 1) * P],
                                          const[:, C_IDENT:C_IDENT + P])
                    mm.then_inc(xn2_t, 1)
                if prep:
                    pe.wait_ge(shifts_ready, n + 1)
                    wait(pe, pv_read, 2 * n)
                    for i in range(NG * NWIN):
                        mm = pe.transpose(pv16[AUX:ROWS_ALL, i * W:(i + 1) * W], shifts[:, i, :], ident16[:, :])
                    mm.then_inc(shifts_t, 1)
                if attn:
                    pe.wait_ge(xt_hi_ready, t + 1)
                    pe.wait_ge(xt_lo_ready, t + 1)
                    for c in range(KC):
                        for i, xs in enumerate((xt_hi, xt_lo)):
                            mm = pe.matmul(misc[:, 0:THIRDS * E], xs[:, par, c, :],
                                           wg_thirds[:, c, :, :].rearrange("p q e -> p (q e)"),
                                           start=(c == 0 and i == 0), stop=(c == KC - 1 and i == 1))
                    mm.then_inc(logits, 1)

            steps(pe, step)

        @block.scalar
        def _(act):
            act.sem_inc(relu_done, START)
            act.wait_ge(s_wt, 2)
            act.activation(wv_t[:, :], pv[:, 0:DK], ACT.Copy).then_inc(s_wt_copied, 1)
            act.wait_ge(small_in, 16 * 8)
            act.activation(tg, g2, ACT.Tanh).then_inc(s_tanh, 1)
            act.wait_ge(s_tanh, 1)
            act.wait_ge(s_wt, 3)
            act.activation(wo_t[:, :], ffn_bank[0][0:DK, 0:P], ACT.Copy, scale=tg[0:DK, 0:1]).then_inc(s_wt_copied, 1)

            def step(t, par, ffn, attn, prep):
                n, npar = t + 1, (par + 1) % 2
                f, fpar = t - 1, (par + 1) % 2

                def relu(e):
                    if not ffn:
                        return
                    act.wait_ge(biased, E * f + e + 1)
                    if e == 0:
                        act.wait_ge(gates_ready, f + 1)
                        act.wait_ge(out_done[fpar], 16 * START + 8 * (f - fpar))
                        to = total[:, fpar, :]
                    else:
                        act.wait_ge(summed, START + (E - 1) * f + max(e - 2, 0))
                        to = expert_out[:, e % 2, :]
                    act.activation(to, ffn_bank[e % 2][:, :], ACT.Relu, scale=gate[:, fpar, e:e + 1]).then_inc(relu_done, 1)

                def exp(w):
                    if not attn:
                        return
                    act.wait_ge(scores_t, NWIN * t + w + 1)
                    wait(act, lo_done, NWIN * t + w - 1)
                    wait(act, pv_done, NWIN * t + w - 1)
                    act.activation(prob_hi[:, w % 2, :], score[w % 2][:, :], ACT.Exp, scale=exp_scale).then_inc(hi_done, 1)
                    act.activation(prob32[:, w % 2, :], score[w % 2][:, :], ACT.Exp, scale=exp_scale).then_inc(exp_done, 1)

                exp(0)
                if prep:
                    act.wait_ge(qk_proj, n + 1)
                    wait(act, lo_ready, n)
                    if isinstance(n, int) and n == 0:
                        act.wait_ge(s_scale, 2)
                    act.activation(qk32[:, :], misc[:, :], ACT.Identity, bias=bias_qk, scale=scale_qk).then_inc(qk_scaled, 1)
                    act.wait_ge(k_masked, n + 1)
                    wait(act, stacks_in, 16 * STACK_DMAS * n)
                    act.activation(qk_hi[:, :], qk32[:, :], ACT.Copy).then_inc(hi_ready, 1)
                exp(1)
                relu(0)
                exp(2)
                relu(1)
                exp(3)
                relu(2)
                relu(3)
                relu(4)
                if attn:
                    act.wait_ge(o_t, t + 1)
                    wait(act, wo_done, t)
                    act.activation(o_gelu[:, :], misc[0:DK, :], ACT.Gelu).then_inc(gelu_done, 1)
                relu(5)
                relu(6)
                relu(7)
                if attn:
                    act.wait_ge(xn2_t, t + 1)
                    wait(act, ffn_done, START + E * (t - 1))
                    act.activation(xt_hi[:, par, :, :].rearrange("p c t -> p (c t)"), misc[:, :],
                                   ACT.Copy).then_inc(xt_hi_ready, 1)
                if prep:
                    act.wait_ge(shifts_t, n + 1)
                    if isinstance(n, int) and n == 0:
                        act.wait_ge(s_init, 4)
                    act.activation(q_stack[AUX:ROWS_ALL, npar, :, :].rearrange("p g s -> p (g s)"),
                                   pv16[AUX:ROWS_ALL, :], ACT.Copy).then_inc(shift_rows, 1)

            steps(act, step)

        @block.vector
        def _(dve):
            dve.memset(half_neg[:, :], -0.5).then_inc(s_init, 1)
            dve.memset(q_stack[AUX:P, :, :, :], MASK_Q).then_inc(s_init, 1)
            dve.memset(shifts[:, :, 0:1], MASK_Q).then_inc(s_init, 1)
            dve.memset(v_thirds[:, :, :, :, DH:VC], 0.0).then_inc(s_init, 1)
            dve.wait_ge(s_init, 4)
            dve.memset(v_thirds[:, :, :, 0, DH:VC], 1.0).then_inc(s_init, 1)
            dve.wait_ge(x0_in, 16)
            dve.bn_stats(stats1[:, 0, :], x_all[:, 0, :]).then_inc(s_stat, 1)
            dve.wait_ge(s_stat, 1)
            dve.bn_aggr(mean_var1[:, 0, :], stats1[:, 0, :]).then_inc(s_stat, 1)
            dve.wait_ge(s_stat, 2)
            dve.tensor_scalar(rstd1[:, 0, 0:1], mean_var1[:, 0, 1:2], EPS, None, ALU.add).then_inc(s_var1, 1)
            dve.wait_ge(s_wt, 1)
            dve.tensor_copy(wqk_t[:, :], misc[:, 0:P]).then_inc(s_wt_copied, 1)
            dve.wait_ge(const_in, 16)
            dve.tensor_copy(ident16[:, :], const[:, C_IDENT:C_IDENT + P]).then_inc(s_ident, 1)
            dve.wait_ge(wqk_in, 32)
            dve.tensor_reduce(qk_small[:, 0:1], w_rows[:, 0, :], AX.X, ALU.add, apply_absolute_value=True).then_inc(s_sums, 1)
            dve.wait_ge(small_in, 16 * 8)
            dve.tensor_reduce(qk_small[:, 1:2], bqk, AX.X, ALU.max, apply_absolute_value=True).then_inc(s_sums, 1)
            dve.wait_ge(s_sums, 2)
            dve.tensor_scalar(bound, qk_small[:, 0:1], NORM_BOUND, qk_small[:, 1:2], ALU.mult, ALU.add).then_inc(s_sums, 1)
            dve.wait_ge(s_sums, 3)
            dve.tensor_scalar(qk_small[:, 2:4], const[:, C_SIDE:C_SIDE + 2], bound, QK_FLOOR, ALU.mult, ALU.max).then_inc(s_sums, 1)
            dve.wait_ge(s_bound, 1)
            dve.tensor_scalar(qk_small[:, 4:6].bitcast(I32), qk_small[:, 4:6].bitcast(I32), 0x7F800000, None,
                              ALU.bitwise_and).then_inc(s_sums, 1)
            dve.wait_ge(s_sums, 5)
            dve.reciprocal(qk_small[:, 6:8], qk_small[:, 4:6]).then_inc(s_sums, 1)
            dve.tensor_scalar(exp_scale, qk_small[:, 4:5], qk_small[:, 5:6], float(DH) ** -0.5 / QK_TOP ** 2,
                              ALU.mult, ALU.mult).then_inc(s_sums, 1)
            dve.wait_ge(s_sums, 7)
            dve.tensor_scalar(scale_qk[0:DK, :], qk_small[0:DK, 6:7], QK_TOP, None, ALU.mult).then_inc(s_sums, 1)
            dve.tensor_scalar(scale_qk[DK:2 * DK, :], qk_small[DK:2 * DK, 7:8], QK_TOP, None, ALU.mult).then_inc(s_scale, 1)
            dve.wait_ge(s_sums, 8)
            dve.wait_ge(s_scale, 1)
            dve.tensor_tensor(bias_qk, bqk, scale_qk, ALU.mult).then_inc(s_scale, 1)
            dve.wait_ge(s_tanh, 1)
            dve.tensor_tensor(bo_c, bo_c, tg[:, 0:1], ALU.mult).then_inc(s_wot, 1)
            dve.tensor_copy(wg_thirds[:, :, 0, :], wg_in[:, :, :]).then_inc(s_wg, 1)
            dve.wait_ge(s_wg, 1)
            dve.tensor_tensor(wg_rest[:, :, :], wg_in[:, :, :], wg_thirds[:, :, 0, :], ALU.subtract).then_inc(s_wg, 1)
            dve.wait_ge(s_wg, 2)
            dve.tensor_copy(wg_thirds[:, :, 1, :], wg_rest[:, :, :]).then_inc(s_wg, 1)
            dve.wait_ge(s_wg, 3)
            dve.tensor_tensor(wg_thirds[:, :, 2, :], wg_rest[:, :, :], wg_thirds[:, :, 1, :], ALU.subtract).then_inc(s_wg, 1)

            def rest_of_norms():
                dve.wait_ge(xrest_in, 16 * (B - 1))
                for b in range(1, B):
                    dve.bn_stats(stats1[:, b, :], x_all[:, b, :]).then_inc(s_stat, 1)
                for b in range(1, B):
                    dve.wait_ge(s_stat, 2 + b)
                    dve.bn_aggr(mean_var1[:, b, :], stats1[:, b, :]).then_inc(s_stat, 1)
                dve.wait_ge(s_stat, 2 * B)
                dve.tensor_scalar(rstd1[:, 1:B, 0], mean_var1[:, 1:B, 1], EPS, None, ALU.add).then_inc(s_var1, 1)

            def expert_scale(e):
                dve.wait_ge(we_loaded[e % 2], 16 * (e // 2 + 1))
                dve.tensor_reduce(we_amax[:, e:e + 1], we_in[:, e % 2, :, :].rearrange("p k s -> p (k s)"),
                                  AX.X, ALU.max, apply_absolute_value=True).then_inc(s_amax, 1)

            def expert_split(e):
                one = slice(e, e + 1)
                dve.wait_ge(s_amax_all, e + 1)
                dve.tensor_scalar(we_pow[:, one], we_amax_all[:, one], 2.0 ** -100, None, ALU.max).then_inc(s_wscale, 1)
                dve.wait_ge(s_wscale, 5 * e + 1)
                dve.tensor_scalar(we_pow[:, one].bitcast(I32), we_pow[:, one].bitcast(I32), 0x7F800000, None,
                                  ALU.bitwise_and).then_inc(s_wscale, 1)
                dve.wait_ge(s_wscale, 5 * e + 2)
                dve.reciprocal(we_scale[:, one], we_pow[:, one]).then_inc(s_wscale, 1)
                dve.tensor_scalar(we_unscale[:, one], we_pow[:, one], 0.5 / WE_TOP, None, ALU.mult).then_inc(s_wscale, 1)
                dve.wait_ge(s_wscale, 5 * e + 3)
                dve.tensor_scalar(we_scale[:, one], we_scale[:, one], WE_TOP, None, ALU.mult).then_inc(s_wscale, 1)
                if e == 0:
                    dve.wait_ge(bias_in, 16)
                dve.wait_ge(s_wscale, 5 * e + 5)
                dve.tensor_scalar(expert_bias[:, e, :], expert_bias[:, e, :], we_scale[:, one], None, ALU.mult).then_inc(s_ebias, 1)
                dve.wait_ge(s_whi, e + 1)
                flat = "p k s -> p (k s)"
                dve.scalar_tensor_tensor(we_lo[:, e, :, :].rearrange(flat), we_in[:, e % 2, :, :].rearrange(flat),
                                         we_scale[:, one], we_hi[:, e, :, :].rearrange(flat),
                                         ALU.mult, ALU.subtract).then_inc(s_wlo, 1)

            def step(t, par, ffn, attn, prep):
                n, npar = t + 1, (par + 1) % 2
                f, fpar = t - 1, (par + 1) % 2
                first = isinstance(t, int) and t == 0
                start = isinstance(t, int) and t == -1

                def add_bias(e):
                    if not ffn:
                        if first:
                            if e + 1 < E:
                                expert_scale(e + 1)
                            expert_split(e)
                        return
                    dve.wait_ge(ffn_done, START + E * f + e + 1)
                    dve.tensor_tensor(ffn_bank[e % 2][:, :], ffn_bank[e % 2][:, :], expert_bias[:, e, :],
                                      ALU.add).then_inc(biased, 1)

                def low_half(w):
                    if not attn:
                        return
                    dve.wait_ge(exp_done, NWIN * t + w + 1)
                    wait(dve, pv_done, NWIN * t + w - 1)
                    dve.tensor_tensor(prob_lo[:, w % 2, :], prob32[:, w % 2, :], prob_hi[:, w % 2, :],
                                      ALU.subtract).then_inc(lo_done, 1)

                def maxima(w):
                    if not prep:
                        return
                    dve.wait_ge(scores, NWIN * n + w + 1)
                    dve.tensor_reduce(row_max[:, :, w, :], score[w % 2][:, :].rearrange("p (g h j) -> p g h j", g=NG, h=HG),
                                      AX.X, ALU.max).then_inc(max_done, 1)

                def add_windows(half):
                    if not attn:
                        return
                    dve.wait_ge(pv_done, NWIN * t + 2 * half + 2)
                    n_in = 2 * H
                    dve.tensor_reduce(o_sum[:, half * n_in:(half + 1) * n_in, :],
                                      pv[:, 0:n_in * THIRDS * VC].rearrange("p (x q c) -> p x c q", q=THIRDS, c=VC),
                                      AX.X, ALU.add).then_inc(pv_read, 1)

                if start:
                    expert_scale(0)
                if prep:
                    if start:
                        dve.wait_ge(s_rstd1, 1)
                    if first:
                        dve.wait_ge(s_rstd1, 2)
                    wait(dve, qk_proj, n)
                    dve.tensor_scalar(xn[:, :], x_all[:, n, :], mean_var1[:, n, 0:1], rstd1[:, n, 1:2],
                                      ALU.subtract, ALU.mult).then_inc(xn_ready, 1)
                    if start:
                        dve.wait_ge(mask_in, 16)
                    dve.tensor_scalar(k_rows[AUX:P, :, :], mask_all[AUX:P, n, :].unsqueeze(1).broadcast_to([P - AUX, NG, S]),
                                      0.0, -AUX_K, ALU.is_le, ALU.mult).then_inc(mask_row, 1)
                    dve.wait_ge(qk_scaled, n + 1)
                    dve.scalar_tensor_tensor(qk32[DK:2 * DK, :], mask_all[DK:2 * DK, n, :], 0.0, qk32[DK:2 * DK, :],
                                             ALU.is_gt, ALU.mult).then_inc(k_masked, 1)
                    dve.wait_ge(hi_ready, n + 1)
                    wait(dve, stacks_in, 16 * STACK_DMAS * n)
                    dve.tensor_tensor(qk_lo[:, :], qk32[:, :], qk_hi[:, :], ALU.subtract).then_inc(lo_ready, 1)
                low_half(0)
                add_bias(0)
                if prep:
                    dve.wait_ge(v_proj, n + 1)
                    wait(dve, v_ready, n)
                    dve.tensor_tensor(v32[:, :, :].rearrange("p (w h) d -> p w (h d)", w=NWIN),
                                      misc[:, 0:NWIN * DK].rearrange("p (w c) -> p w c", w=NWIN),
                                      bv_b[:, :].unsqueeze(1).broadcast_to([P, NWIN, DK]), ALU.add).then_inc(v_biased, 1)
                low_half(1)
                add_bias(1)
                add_windows(0)
                low_half(2)
                add_bias(2)
                low_half(3)
                if start:
                    rest_of_norms()
                if prep:
                    dve.wait_ge(stacks_in, 16 * STACK_DMAS * (n + 1))
                    dve.wait_ge(mask_row, n + 1)
                    wait(dve, scores_t, NWIN * (n - 1))
                    for h in range(HG):
                        mm = dve.tensor_scalar(k_stack[:, npar, :, h, :], k_rows[:, :, :], const[:, C_HEAD + h:C_HEAD + h + 1],
                                               const[:, C_ONE + h:C_ONE + h + 1], ALU.mult, ALU.add)
                    mm.then_inc(k_ready, 1)
                add_bias(3)
                maxima(0)
                if attn:
                    add_windows(1)
                    dve.wait_ge(pv_read, 2 * t + 2)
                    dve.reciprocal(o_den[:, :], o_sum[:, :, DH]).then_inc(den_ready, 1)
                    dve.wait_ge(den_ready, t + 1)
                    wait(dve, o_t, t)
                    dve.tensor_tensor(o_norm[:, :, :], o_sum[:, :, 0:DH],
                                      o_den[:, :].unsqueeze(2).broadcast_to([P, NWIN * H, DH]), ALU.mult).then_inc(o_ready, 1)
                add_bias(4)
                maxima(1)
                add_bias(5)
                maxima(2)
                if attn:
                    dve.wait_ge(wo_done, t + 1)
                    if first:
                        dve.wait_ge(s_wot, 1)
                    dve.scalar_tensor_tensor(attn_out[:, :], misc[:, :], bo_c, mask_all[:, t, :], ALU.add,
                                             ALU.mult).then_inc(attn_masked, 1)
                    dve.wait_ge(attn_masked, t + 1)
                    dve.tensor_tensor(x_all[:, t, :], x_all[:, t, :], attn_out[:, :], ALU.add).then_inc(x1_ready, 1)
                    wait_alone(dve, (x1_ready, t + 1))
                    dve.bn_stats(stats2[:, :], x_all[:, t, :]).then_inc(s_stat2, 1)
                    wait_alone(dve, (s_stat2, 2 * t + 1))
                    dve.bn_aggr(mean_var2[:, 0:2], stats2[:, :]).then_inc(s_stat2, 1)
                    dve.wait_ge(s_stat2, 2 * t + 2)
                    dve.tensor_scalar(mean_var2[:, 2:3], mean_var2[:, 1:2], EPS, None, ALU.add).then_inc(s_var2, 1)
                    dve.wait_ge(s_rstd2, t + 1)
                    wait(dve, xn2_t, t)
                    dve.tensor_scalar(xn2[:, :], x_all[:, t, :], mean_var2[:, 0:1], mean_var2[:, 3:4],
                                      ALU.subtract, ALU.mult).then_inc(xn2_ready, 1)
                add_bias(6)
                maxima(3)
                if prep:
                    dve.wait_ge(max_done, NWIN * (n + 1))
                    wait(dve, shifts_t, n)
                    m = row_max[:, :, :, :].rearrange("p g w h -> p (g w) h")
                    dve.tensor_scalar(shifts[:, :, 1:1 + HG], m, -1.0 / AUX_K, None, ALU.mult).then_inc(max_hi, 1)
                    dve.wait_ge(max_hi, n + 1)
                    dve.scalar_tensor_tensor(shifts[:, :, 1 + HG:1 + 2 * HG], m, -1.0 / AUX_K, shifts[:, :, 1:1 + HG],
                                             ALU.mult, ALU.subtract).then_inc(shifts_ready, 1)
                add_bias(7)
                if attn:
                    dve.wait_ge(xt_hi_ready, t + 1)
                    dve.tensor_tensor(xt_lo[:, par, :, :].rearrange("p c t -> p (c t)"), misc[:, :],
                                      xt_hi[:, par, :, :].rearrange("p c t -> p (c t)"), ALU.subtract).then_inc(xt_lo_ready, 1)
                    dve.wait_ge(logits, t + 1)
                    dve.tensor_reduce(logit[:, 0, :], misc[:, 0:THIRDS * E].rearrange("p (q e) -> p e q", q=THIRDS),
                                      AX.X, ALU.add).then_inc(logits_read, 1)
                    dve.wait_ge(logits_read, t + 1)
                    dve.tensor_tensor(logit[:, 1, :], logit[:, 0, :], bg_b[:, :], ALU.add).then_inc(s_gate, 1)
                    dve.wait_ge(s_gate, 7 * t + 1)
                    other = logit[:, 1, :].unsqueeze(1).broadcast_to([P, E, E])
                    own = logit[:, 1, :].unsqueeze(2).broadcast_to([P, E, E])
                    earlier = const[:, C_EARLIER:C_EARLIER + E * E].rearrange("p (e j) -> p e j", e=E)
                    dve.tensor_tensor(pairs[:, 0, :, :], other, own, ALU.is_gt).then_inc(s_gate, 1)
                    dve.tensor_tensor(pairs[:, 1, :, :], other, own, ALU.is_equal).then_inc(s_gate, 1)
                    dve.wait_ge(s_gate, 7 * t + 3)
                    dve.tensor_tensor(pairs[:, 1, :, :], pairs[:, 1, :, :], earlier, ALU.mult).then_inc(s_gate, 1)
                    dve.tensor_reduce(rank[:, 0, :], pairs[:, 0, :, :], AX.X, ALU.add).then_inc(s_gate, 1)
                    dve.wait_ge(s_gate, 7 * t + 4)
                    dve.tensor_reduce(rank[:, 1, :], pairs[:, 1, :, :], AX.X, ALU.add).then_inc(s_gate, 1)
                    dve.wait_ge(s_gate, 7 * t + 6)
                    dve.tensor_tensor(rank[:, 0, :], rank[:, 0, :], rank[:, 1, :], ALU.add).then_inc(s_gate, 1)
                    dve.wait_ge(s_gate, 7 * t + 7)
                    wait(dve, relu_done, START + E * (t - 1))
                    dve.scalar_tensor_tensor(gate[:, par, :], rank[:, 0, :], 1.5, we_unscale[:, :], ALU.is_lt,
                                             ALU.mult).then_inc(gates_ready, 1)
                if ffn:
                    dve.wait_ge(summed, START + (E - 1) * (f + 1))
                    dve.scalar_tensor_tensor(total[:, fpar, :], total[:, fpar, :], tg[:, 1:2], x_all[:, f, :],
                                             ALU.mult, ALU.add).then_inc(out_ready, 1)

            steps(dve, step)

        @block.gpsimd
        def _(pool):
            def load_expert(e):
                pool.dma_start(we_in[:, e % 2, :, :],
                               w_e[e].rearrange("(k p) s -> p k s", p=P)).then_inc(we_loaded[e % 2], 16)

            def expert_hi(e):
                pool.wait_ge(s_amax, e + 1)
                pool.partition_all_reduce(we_amax_all[:, e:e + 1], we_amax[:, e:e + 1], P, MAXIMUM).then_inc(s_amax_all, 1)
                pool.wait_ge(s_wscale, 5 * e + 5)
                flat = "p k s -> p (k s)"
                pool.tensor_scalar(we_hi[:, e, :, :].rearrange(flat), we_in[:, e % 2, :, :].rearrange(flat),
                                   we_scale[:, e:e + 1], 1.0, ALU.mult, ALU.mult).then_inc(s_whi, 1)
                if e + 2 < E:
                    pool.wait_ge(s_wlo, e + 1)
                    load_expert(e + 2)

            pool.sem_inc(summed, START)
            load_expert(0)
            load_expert(1)
            pool.wait_ge(s_init, 1)
            pool.wait_ge(s_var1, 1)
            pool.tensor_tensor(rstd1[:, 0, 1:2], rstd1[:, 0, 0:1], half_neg[:, :], ALU.pow).then_inc(s_rstd1, 1)
            pool.wait_ge(s_sums, 4)
            pool.partition_all_reduce(qk_small[:, 4:6], qk_small[:, 2:4], P, MAXIMUM).then_inc(s_bound, 1)

            def step(t, par, ffn, attn, prep):
                n, npar = t + 1, (par + 1) % 2
                f, fpar = t - 1, (par + 1) % 2
                first = isinstance(t, int) and t == 0

                def accumulate(e):
                    if not ffn:
                        if first:
                            expert_hi(e)
                        return
                    if e == 0:
                        return
                    pool.wait_ge(relu_done, START + E * f + e + 1)
                    pool.wait_ge(summed, START + (E - 1) * f + e - 1)
                    pool.tensor_tensor(total[:, fpar, :], total[:, fpar, :], expert_out[:, e % 2, :],
                                       ALU.add).then_inc(summed, 1)

                accumulate(0)
                if prep:
                    thirds = v_thirds[:, npar, :, :, :]
                    wait_alone(pool, (v_biased, n + 1), (pv_done, NWIN * (n - 1)))
                    if isinstance(n, int) and n == 0:
                        pool.wait_ge(s_init, 5)
                    pool.tensor_copy(thirds[:, :, 0, 0:DH], v32[:, :, :]).then_inc(v_step, 1)
                    pool.wait_ge(v_step, 4 * n + 1)
                    pool.tensor_tensor(v32[:, :, :], v32[:, :, :], thirds[:, :, 0, 0:DH], ALU.subtract).then_inc(v_step, 1)
                    wait_alone(pool, (v_step, 4 * n + 2))
                    pool.tensor_copy(thirds[:, :, 1, 0:DH], v32[:, :, :]).then_inc(v_step, 1)
                    pool.wait_ge(v_step, 4 * n + 3)
                    pool.tensor_tensor(v32[:, :, :], v32[:, :, :], thirds[:, :, 1, 0:DH], ALU.subtract).then_inc(v_step, 1)
                    wait_alone(pool, (v_step, 4 * n + 4))
                    pool.tensor_copy(thirds[:, :, 2, 0:DH], v32[:, :, :]).then_inc(v_ready, 1)
                if isinstance(t, int) and t == -1:
                    pool.wait_ge(s_var1, 2)
                    pool.tensor_tensor(rstd1[:, 1:B, 1], rstd1[:, 1:B, 0], half_neg[:, :].broadcast_to([P, B - 1]),
                                       ALU.pow).then_inc(s_rstd1, 1)
                accumulate(1)
                accumulate(2)
                accumulate(3)
                accumulate(4)
                accumulate(5)
                if attn:
                    pool.wait_ge(s_var2, t + 1)
                    pool.tensor_tensor(mean_var2[:, 3:4], mean_var2[:, 2:3], half_neg[:, :], ALU.pow).then_inc(s_rstd2, 1)
                accumulate(6)
                accumulate(7)

            steps(pool, step)


_INS = ["x", "ctx_4096", "mask_Bx1x4096_ff1", "g_xattn", "g_ffn", "L0_xattn_Wq", "L0_xattn_bq", "L0_xattn_Wk",
        "L0_xattn_bk", "L0_xattn_Wv", "L0_xattn_bv", "L0_xattn_Wo", "L0_xattn_bo", "L0_ffn_W_gate",
        "L0_ffn_b_gate", "L0_ffn_W_e", "L0_ffn_b_e"]


def kernel(**inputs):
    import numpy as np
    import concourse.bacc as bacc
    from concourse.bass_utils import run_bass_kernel_spmd as run

    nc = bacc.Bacc("TRN2", target_bir_lowering=False, num_devices=1)
    arrays, args = {}, []
    for name in _INS:
        a = np.ascontiguousarray(inputs[name])
        arrays[f"in_{name}"] = a
        args.append(nc.dram_tensor(f"in_{name}", a.shape, mybir.dt.from_np(a.dtype), kind="ExternalInput").ap())
    arrays["in_constants"] = shape_constants()
    args.append(nc.dram_tensor("in_constants", (P, C_END), F32, kind="ExternalInput").ap())
    args.append(nc.dram_tensor("out_0", (B, D, S), F32, kind="ExternalOutput").ap())
    build(nc, *args)
    return run(nc, [arrays], core_ids=[0]).results[0]["out_0"]
```

```python
from contextlib import ExitStack

import concourse.bass as bass
from concourse import mybir

F32 = mybir.dt.float32
F16 = mybir.dt.float16
BF16 = mybir.dt.bfloat16
I32 = mybir.dt.int32
ALU = mybir.AluOpType
ACT = mybir.ActivationFunctionType
AX = mybir.AxisListType

START = 1
MAXIMUM = bass.bass_isa.ReduceOp.max

P = 128
B, D, S = 8, 128, 512
W = 128
NWIN = S // W
H, DH = 8, 8
DK = H * DH
NG = 2
HG = H // NG
QUAD = HG * DH
E = 8
KC = S // P
EPS = 1e-5
NORM_BOUND = 22.7
QK_FLOOR = 8.0
QK_TOP = 2.0 ** 11
WE_TOP = 2.0 ** 14
AUX = 3 * QUAD
ROWS_MASK = AUX + 1
ROWS_ALL = AUX + 1 + 2 * HG
MASK_Q = 2.0 ** 15
AUX_K = 2.0 ** 14
THIRDS = 3
EARLY = 3
VC = DH + 1
WE_BUFS = 3
STACK_DMAS = 12

C_IDENT = 0
C_HEAD = C_IDENT + P
C_ONE = C_HEAD + HG
C_EARLIER = C_ONE + HG
C_SIDE = C_EARLIER + E * E
C_END = C_SIDE + 2


def shape_constants():
    import numpy as np

    c = np.zeros((P, C_END), np.float32)
    c[:, C_IDENT:C_IDENT + P] = np.eye(P)
    for h in range(HG):
        for third in range(3):
            at = third * QUAD + h * DH
            c[at:at + DH, C_HEAD + h] = 1
        c[AUX, C_HEAD + h] = 1
        c[AUX + 1 + h, C_ONE + h] = AUX_K
        c[AUX + 1 + HG + h, C_ONE + h] = AUX_K
    for e in range(E):
        for j in range(e):
            c[:, C_EARLIER + e * E + j] = 1
    c[0:DK, C_SIDE] = 1
    c[DK:2 * DK, C_SIDE + 1] = 1
    return c


def build(nc, x, ctx_in, mask, g_xattn, g_ffn, wq, bq, wk, bk, wv, bv, wo, bo,
          w_gate, b_gate, w_e, b_e, consts, out):
    stack = ExitStack()
    with stack:
        def sb(name, shape, dt=F32):
            return stack.enter_context(nc.sbuf_tensor(name, shape, dt))

        def pb(name, shape, dt=F32):
            return stack.enter_context(nc.psum_tensor(name, shape, dt))

        def sem(name):
            return stack.enter_context(nc.semaphore(name))

        x_all = sb("x_all", [P, B, S])
        mask_all = sb("mask_all", [P, B, S])
        expert_bias = sb("expert_bias", [P, E, S])
        we_in = sb("we_in", [P, 2, KC, S])
        work = sb("work", [P, 4, S])
        total, expert_out = work[:, 0:2, :], work[:, 2:4, :]
        we_hi = sb("we_hi", [P, E, KC, S], F16)
        we_lo = sb("we_lo", [P, E, KC, S], F16)
        ctx_sb = sb("ctx_sb", [P, 2, S])
        const = sb("const", [P, C_END])
        w_rows = sb("w_rows", [P, 4, P])
        wqk_t = sb("wqk_t", [P, P])
        wv_t = sb("wv_t", [P, DK])
        wo_t = sb("wo_t", [DK, P])
        bv_c = sb("bv_c", [P, 1])
        wg_in = sb("wg_in", [P, KC, E])
        wg_rest = sb("wg_rest", [P, KC, E])
        wg_thirds = sb("wg_thirds", [P, KC, THIRDS, E], BF16)
        ident16 = sb("ident16", [P, P], F16)
        col = sb("col", [P, 16])
        bqk, bo_c, g2, tg, scale_qk = col[:, 0:1], col[:, 1:2], col[:, 2:4], col[:, 4:6], col[:, 6:7]
        bias_qk, exp_scale, bound, zero_c = col[:, 7:8], col[:, 8:9], col[:, 9:10], col[:, 10:11]
        half_neg = sb("half_neg", [P, 1])
        bg_b = sb("bg_b", [P, E])
        qk_small = sb("qk_small", [P, 8])
        we_bound = sb("we_bound", [P, E])
        we_bound_all = sb("we_bound_all", [P, E])
        we_pow = sb("we_pow", [P, E])
        we_scale = sb("we_scale", [P, E])
        we_unscale = sb("we_unscale", [P, E])

        stats1 = sb("stats1", [P, B, 6])
        mean_var1 = sb("mean_var1", [P, B, 2])
        rstd1 = sb("rstd1", [P, B, 2])
        shift1 = sb("shift1", [P, B, 1])
        xn = sb("xn", [P, S])
        qk32 = sb("qk32", [P, S])
        qk_hi = sb("qk_hi", [P, S], F16)
        qk_lo = sb("qk_lo", [P, S], F16)
        q_stack = sb("q_stack", [P, 2, NG, S], F16)
        k_rows = sb("k_rows", [P, NG, S], F16)
        k_stack = sb("k_stack", [P, 2, NG, HG, S], F16)
        row_max = sb("row_max", [P, NG, NWIN, HG])
        shifts = sb("shifts", [P, NG * NWIN, 1 + 2 * HG], F16)
        prob32 = sb("prob32", [P, 2, H * W])
        prob_hi = sb("prob_hi", [P, 2, H * W], F16)
        prob_lo = sb("prob_lo", [P, 2, H * W], F16)
        v32 = sb("v32", [P, NWIN * H, DH])
        v_thirds = sb("v_thirds", [P, 2, NWIN * H, THIRDS, VC], BF16)
        o_sum = sb("o_sum", [P, NWIN * H, VC])
        o_den = sb("o_den", [P, NWIN * H])
        o_norm = sb("o_norm", [P, NWIN * H, DH])
        o_gelu = sb("o_gelu", [DK, S])
        attn_out = sb("attn_out", [P, S])

        stats2 = sb("stats2", [P, 6])
        mean_var2 = sb("mean_var2", [P, 4])
        xn2 = sb("xn2", [P, S])
        xt_hi = sb("xt_hi", [P, 2, KC, P], F16)
        xt_lo = sb("xt_lo", [P, 2, KC, P], F16)
        logit = sb("logit", [P, 2, E])
        pairs = sb("pairs", [P, 2, E, E])
        rank = sb("rank", [P, 2, E])
        gate = sb("gate", [P, 2, E])

        score = [pb(f"score{i}", [P, H * W]) for i in range(2)]
        ffn_bank = [pb(f"ffn{i}", [P, S]) for i in range(2)]
        pv = pb("pv", [P, S])
        misc = pb("misc", [P, S])
        pv16 = pv[:, :].bitcast(F16)

        const_in, wqk_in, x0_in, early_in, xrest_in, mask_early_in, mask_in = map(
            sem, ("const_in", "wqk_in", "x0_in", "early_in", "xrest_in", "mask_early_in", "mask_in"))
        wvo_in, small_in, bias_in = map(sem, ("wvo_in", "small_in", "bias_in"))
        ctx_loaded = [sem(f"ctx_loaded{i}") for i in range(2)]
        we_loaded = [sem(f"we_loaded{i}") for i in range(WE_BUFS)]
        s_ident, s_wt, s_wt_copied, s_sums, s_bound, s_scale, s_tanh = map(
            sem, ("s_ident", "s_wt", "s_wt_copied", "s_sums", "s_bound", "s_scale", "s_tanh"))
        s_wot, s_wg, s_init, s_sum, s_sum_all, s_wscale, s_wlo, s_whi, s_ebias = map(
            sem, ("s_wot", "s_wg", "s_init", "s_sum", "s_sum_all", "s_wscale", "s_wlo", "s_whi", "s_ebias"))
        s_stat, s_var1, s_rstd1, s_shift1 = map(sem, ("s_stat", "s_var1", "s_rstd1", "s_shift1"))
        xn_ready, qk_proj, qk_scaled, k_masked, hi_ready, lo_ready, stacks_in = map(
            sem, ("xn_ready", "qk_proj", "qk_scaled", "k_masked", "hi_ready", "lo_ready", "stacks_in"))
        mask_row, k_ready, v_proj, v_copied, v_step, v_ready = map(
            sem, ("mask_row", "k_ready", "v_proj", "v_copied", "v_step", "v_ready"))
        scores, max_done, max_hi, shifts_ready, shifts_t, shift_rows = map(
            sem, ("scores", "max_done", "max_hi", "shifts_ready", "shifts_t", "shift_rows"))
        scores_t, exp_done, hi_done, lo_done, pv_done = map(
            sem, ("scores_t", "exp_done", "hi_done", "lo_done", "pv_done"))
        pv_read, den_ready, o_ready, o_t, gelu_done, wo_done, attn_masked, x1_ready = map(
            sem, ("pv_read", "den_ready", "o_ready", "o_t", "gelu_done", "wo_done", "attn_masked", "x1_ready"))
        s_stat2, s_var2, s_rstd2, xn2_ready, xn2_t, xt_hi_ready, xt_lo_ready = map(
            sem, ("s_stat2", "s_var2", "s_rstd2", "xn2_ready", "xn2_t", "xt_hi_ready", "xt_lo_ready"))
        logits, logits_read, s_gate, gates_ready = map(sem, ("logits", "logits_read", "s_gate", "gates_ready"))
        ffn_done, biased, relu_done, summed, out_ready = map(
            sem, ("ffn_done", "biased", "relu_done", "summed", "out_ready"))
        out_done = [sem(f"out_done{i}") for i in range(2)]

        flat = "p k s -> p (k s)"

        def part_of_batch(b):
            return 3 if not isinstance(b, int) or b >= EARLY else 2 if b > 0 else 1

        def we_buf(e):
            return (work if e % WE_BUFS == 2 else we_in[:, e % WE_BUFS, :, :]).rearrange(flat)

        block = stack.enter_context(nc.Block())

        def wait(eng, semaphore, value):
            if isinstance(value, int) and value <= 0:
                return
            eng.wait_ge(semaphore, value)

        def wait_alone(eng, *waits):
            for _, value in waits:
                if not isinstance(value, int):
                    eng.lower_val(value)
            eng.wait_ge(const_in, 16)
            for semaphore, value in waits:
                wait(eng, semaphore, value)

        def steps(eng, step):
            step(-2, 0, proj=True)
            step(-1, 1, prep=True, proj=True)
            step(0, 0, attn=True, prep=True, proj=True)
            step(1, 1, ffn=True, attn=True, prep=True, proj=True)
            with eng.Fori(1, B // 2 - 1) as i:
                step(2 * i, 0, late=True, ffn=True, attn=True, prep=True, proj=True)
                step(2 * i + 1, 1, late=True, ffn=True, attn=True, prep=True, proj=True)
            step(B - 2, 0, late=True, ffn=True, attn=True, prep=True)
            step(B - 1, 1, late=True, ffn=True, attn=True)
            step(B, 0, late=True, ffn=True)
            step(B + 1, 1, late=True)

        @block.sync
        def _(sp):
            for half in out_done:
                sp.sem_inc(half, 16 * START)
            def column(to, vector):
                sp.dma_start(to, vector.rearrange("(e o) -> e o", o=1)).then_inc(small_in, 16)

            def on_all(to, vector):
                sp.dma_start(to, vector.rearrange("(o e) -> o e", o=1).broadcast_to(to.shape)).then_inc(small_in, 16)

            sp.dma_start(x_all[:, 0, :], x[0]).then_inc(x0_in, 16)
            sp.dma_start(w_rows[0:DK, 0, :], wq).then_inc(wqk_in, 16)
            sp.dma_start(w_rows[DK:2 * DK, 0, :], wk).then_inc(wqk_in, 16)
            sp.dma_start(const[:, :], consts).then_inc(const_in, 16)
            column(bqk[0:DK, :], bq)
            column(bqk[DK:2 * DK, :], bk)
            column(bo_c, bo)
            column(bv_c[0:DK, :], bv)
            on_all(g2[:, 0:1], g_xattn)
            on_all(g2[:, 1:2], g_ffn)
            on_all(bg_b[:, :], b_gate)
            sp.dma_start(wg_in[:, :, :], w_gate.rearrange("(k p) e -> p k e", p=P)).then_inc(small_in, 16)
            sp.dma_start(w_rows[0:DK, 1, :], wv).then_inc(wvo_in, 16)
            sp.dma_start(w_rows[:, 2, 0:DK], wo).then_inc(wvo_in, 16)
            sp.dma_start(mask_all[:, 0:EARLY, :],
                         mask[0:EARLY].rearrange("b o s -> o b s").broadcast_to([P, EARLY, S])).then_inc(mask_early_in, 16)
            sp.dma_start(ctx_sb[:, 0, :], ctx_in[0]).then_inc(ctx_loaded[0], 16)
            for b in range(1, EARLY):
                sp.dma_start(x_all[:, b, :], x[b]).then_inc(early_in, 16)

            def step(t, par, late=False, ffn=False, attn=False, prep=False, proj=False):
                if prep and not (isinstance(t, int) and t == -1):
                    n, npar = t + 1, (par + 1) % 2
                    wait_alone(sp, (v_proj, n - 1))
                    sp.dma_start(ctx_sb[:, npar, :], ctx_in[n]).then_inc(ctx_loaded[npar], 16)
                if proj:
                    m = t + 2
                    wait_alone(sp, (hi_ready, m + 1), (scores_t, NWIN * (t + 1)), (k_ready, m))
                    for third in range(THIRDS):
                        if third == 1:
                            wait_alone(sp, (lo_ready, m + 1))
                        for g in range(NG):
                            q_at, k_at = QUAD * g, DK + QUAD * g
                            rows = slice(QUAD * third, QUAD * (third + 1))
                            sp.dma_start(k_rows[rows, g, :],
                                         (qk_hi, qk_hi, qk_lo)[third][k_at:k_at + QUAD, :]).then_inc(stacks_in, 16)
                            sp.dma_start(q_stack[rows, par, g, :],
                                         (qk_hi, qk_lo, qk_hi)[third][q_at:q_at + QUAD, :]).then_inc(stacks_in, 16)
                if isinstance(t, int) and t == -1:
                    for b in range(EARLY, B):
                        sp.dma_start(x_all[:, b, :], x[b]).then_inc(xrest_in, 16)
                    sp.dma_start(mask_all[:, EARLY:B, :],
                                 mask[EARLY:B].rearrange("b o s -> o b s").broadcast_to([P, B - EARLY, S])
                                 ).then_inc(mask_in, 16)
                    sp.dma_start(expert_bias[:, :, :],
                                 b_e.rearrange("(o e) s -> o e s", o=1).broadcast_to([P, E, S])).then_inc(bias_in, 16)
                if late:
                    wait_alone(sp, (out_ready, t - 1))
                    sp.dma_start(out[t - 2], total[:, par, :]).then_inc(out_done[par], 16)

            steps(sp, step)
            for half in out_done:
                sp.wait_ge(half, 16 * START + 16 * B // 2)

        @block.tensor
        def _(pe):
            pe.sem_inc(ffn_done, START)
            pe.wait_ge(const_in, 16)
            pe.wait_ge(wqk_in, 32)
            ident32 = const[:, C_IDENT:C_IDENT + P]
            pe.transpose(misc[:, 0:P], w_rows[:, 0, :], ident32).then_inc(s_wt, 1)
            pe.wait_ge(wvo_in, 32)
            pe.transpose(pv[:, 0:DK], w_rows[0:DK, 1, :], ident32[0:DK, 0:DK]).then_inc(s_wt, 1)
            pe.transpose(ffn_bank[0][0:DK, 0:P], w_rows[:, 2, 0:DK], ident32).then_inc(s_wt, 1)
            pe.wait_ge(s_wt_copied, 3)

            def score_maxima(n, np_, w):
                slot = score[w % 2]
                if w < 2:
                    wait(pe, exp_done, NWIN * (n - 1) + w + 3)
                else:
                    wait(pe, max_done, NWIN * n + w - 1)
                if w == 0:
                    pe.wait_ge(k_ready, n + 1)
                for g in range(NG):
                    mm = pe.matmul(slot[:, g * HG * W:(g + 1) * HG * W].rearrange("p (h j) -> p h j", h=HG),
                                   q_stack[0:ROWS_MASK, np_, g, w * W:(w + 1) * W],
                                   k_stack[0:ROWS_MASK, np_, g, :, w * W:(w + 1) * W], start=True, stop=True)
                mm.then_inc(scores, 1)

            def score_shifted(t, par, w):
                slot = score[w % 2]
                if w < 2:
                    wait(pe, max_done, NWIN * t + w + 3)
                else:
                    wait(pe, exp_done, NWIN * t + w - 1)
                if w == 0:
                    pe.wait_ge(shift_rows, t + 1)
                for h in range(H):
                    g, hg = h // HG, h % HG
                    mm = pe.matmul(slot[:, h * W:(h + 1) * W],
                                   k_stack[0:ROWS_ALL, par, g, hg, w * W:(w + 1) * W],
                                   q_stack[0:ROWS_ALL, par, g, w * W:(w + 1) * W], start=True, stop=True)
                mm.then_inc(scores_t, 1)

            def weigh_values(t, par, w):
                pe.wait_ge(lo_done, NWIN * t + w + 1)
                if w == 0:
                    pe.wait_ge(v_ready, t + 1)
                if w % 2 == 0:
                    wait(pe, pv_read, 2 * t + w // 2)
                for h in range(H):
                    at = ((w % 2) * H + h) * THIRDS * VC
                    v = v_thirds[:, par, w * H + h, :, :].rearrange("p q c -> p (q c)")
                    for part, half in enumerate((prob_hi, prob_lo)):
                        mm = pe.matmul(pv[:, at:at + THIRDS * VC], half[:, w % 2, h * W:(h + 1) * W], v,
                                       start=(part == 0), stop=(part == 1))
                mm.then_inc(pv_done, 1)

            def expert(f, fpar, e, first):
                if e == 0:
                    pe.wait_ge(xt_hi_ready, f + 1)
                    pe.wait_ge(xt_lo_ready, f + 1)
                if first:
                    pe.wait_ge(s_wlo, e + 1)
                wait(pe, relu_done, START + E * f + e - 1)
                for c in range(KC):
                    for i, (xs, ws) in enumerate(((xt_hi, we_hi), (xt_hi, we_lo), (xt_lo, we_hi))):
                        mm = pe.matmul(ffn_bank[e % 2][:, :], xs[:, fpar, c, :], ws[:, e, c, :],
                                       start=(c == 0 and i == 0), stop=(c == KC - 1 and i == 2))
                mm.then_inc(ffn_done, 1)

            def step(t, par, late=False, ffn=False, attn=False, prep=False, proj=False):
                n, npar = t + 1, (par + 1) % 2
                f, fpar = t - 1, (par + 1) % 2
                first = isinstance(t, int) and t < 3

                def ex(e):
                    if ffn:
                        expert(f, fpar, e, first)

                def ex_late(e):
                    if late:
                        expert(t - 2, par, e, False)

                ex_late(E - 2)
                if ffn:
                    pe.wait_ge(xt_hi_ready, f + 1)
                    pe.wait_ge(xt_lo_ready, f + 1)
                    for c in range(KC):
                        for i, xs in enumerate((xt_hi, xt_lo)):
                            mm = pe.matmul(misc[:, 0:THIRDS * E], xs[:, fpar, c, :],
                                           wg_thirds[:, c, :, :].rearrange("p q e -> p (q e)"),
                                           start=(c == 0 and i == 0), stop=(c == KC - 1 and i == 1))
                    mm.then_inc(logits, 1)
                if attn:
                    score_shifted(t, par, 0)
                    score_shifted(t, par, 1)
                ex_late(E - 1)
                if prep:
                    if isinstance(t, int):
                        pe.wait_ge(ctx_loaded[npar], 16 * (n // 2 + 1))
                    else:
                        pe.wait_ge(ctx_loaded[npar], (n - npar) * 8 + 16)
                    pe.wait_ge(qk_scaled, n + 1)
                    if ffn:
                        pe.wait_ge(logits_read, t)
                    for w in range(NWIN):
                        mm = pe.matmul(misc[:, w * DK:(w + 1) * DK], ctx_sb[:, npar, w * W:(w + 1) * W],
                                       wv_t[:, :], start=True, stop=True)
                    mm.then_inc(v_proj, 1)
                if attn:
                    weigh_values(t, par, 0)
                    score_shifted(t, par, 2)
                ex(0)
                if attn:
                    weigh_values(t, par, 1)
                    score_shifted(t, par, 3)
                if proj:
                    m = t + 2
                    pe.wait_ge(xn_ready, m + 1)
                    wait(pe, v_copied, n + 1)
                    pe.matmul(misc[:, :], wqk_t[:, :], xn[:, :], start=True, stop=True).then_inc(qk_proj, 1)
                ex(1)
                if prep:
                    score_maxima(n, npar, 0)
                if attn:
                    weigh_values(t, par, 2)
                ex(2)
                if prep:
                    score_maxima(n, npar, 1)
                if attn:
                    weigh_values(t, par, 3)
                ex(3)
                if prep:
                    score_maxima(n, npar, 2)
                if attn:
                    if proj:
                        wait_alone(pe, (o_ready, t + 1), (qk_scaled, t + 3))
                    else:
                        wait_alone(pe, (o_ready, t + 1))
                        if prep:
                            pe.wait_ge(v_copied, n + 1)
                        else:
                            pe.wait_ge(logits_read, t)
                    for w in range(NWIN):
                        mm = pe.transpose(misc[0:DK, w * W:(w + 1) * W],
                                          o_norm[:, w * H:(w + 1) * H, :].rearrange("p h d -> p (h d)"),
                                          const[:, C_IDENT:C_IDENT + P])
                    mm.then_inc(o_t, 1)
                if prep:
                    score_maxima(n, npar, 3)
                ex(4)
                if attn:
                    pe.wait_ge(gelu_done, t + 1)
                    pe.matmul(misc[:, :], wo_t[:, :], o_gelu[:, :], start=True, stop=True).then_inc(wo_done, 1)
                ex(5)
                if prep:
                    pe.wait_ge(shifts_ready, n + 1)
                    wait(pe, pv_read, 2 * n)
                    for i in range(NG * NWIN):
                        mm = pe.transpose(pv16[AUX:ROWS_ALL, i * W:(i + 1) * W], shifts[:, i, :], ident16[:, :])
                    mm.then_inc(shifts_t, 1)
                if attn:
                    pe.wait_ge(xn2_ready, t + 1)
                    for c in range(KC):
                        mm = pe.transpose(misc[:, c * P:(c + 1) * P], xn2[:, c * P:(c + 1) * P],
                                          const[:, C_IDENT:C_IDENT + P])
                    mm.then_inc(xn2_t, 1)

            steps(pe, step)

        @block.scalar
        def _(act):
            act.sem_inc(relu_done, START)
            act.wait_ge(s_wt, 2)
            act.activation(wv_t[:, :], pv[:, 0:DK], ACT.Copy).then_inc(s_wt_copied, 1)
            act.wait_ge(small_in, 16 * 8)
            act.activation(tg, g2, ACT.Tanh).then_inc(s_tanh, 1)
            act.wait_ge(s_tanh, 1)
            act.wait_ge(s_wt, 3)
            act.activation(wo_t[:, :], ffn_bank[0][0:DK, 0:P], ACT.Copy, scale=tg[0:DK, 0:1]).then_inc(s_wt_copied, 1)

            def expert_sum(e):
                act.wait_ge(we_loaded[e % WE_BUFS], 16 * (e // WE_BUFS + 1))
                act.activation(we_lo[:, e, :, :].rearrange(flat), we_buf(e), ACT.Abs,
                               accum_out=we_bound[:, e:e + 1]).then_inc(s_sum, 1)

            def step(t, par, late=False, ffn=False, attn=False, prep=False, proj=False):
                n, npar = t + 1, (par + 1) % 2
                f, fpar = t - 1, (par + 1) % 2
                m = t + 2
                pre, start, first = (isinstance(t, int) and t == at for at in (-2, -1, 0))

                def relu(e, fb=f, half=fpar, on=ffn):
                    if not on:
                        return
                    act.wait_ge(biased, E * fb + e + 1)
                    if e == 0:
                        act.wait_ge(gates_ready, fb + 1)
                        act.wait_ge(out_done[half], 16 * START + 8 * (fb - half))
                        to = total[:, half, :]
                    else:
                        act.wait_ge(summed, START + (E - 1) * fb + max(e - 2, 0))
                        to = expert_out[:, e % 2, :]
                    act.activation(to, ffn_bank[e % 2][:, :], ACT.Relu, scale=gate[:, half, e:e + 1]).then_inc(relu_done, 1)

                def normalize(b):
                    act.wait_ge(s_shift1, part_of_batch(b))
                    wait(act, qk_proj, b)
                    act.activation(xn[:, :], x_all[:, b, :], ACT.Identity, bias=shift1[:, b, :],
                                   scale=rstd1[:, b, 1:2]).then_inc(xn_ready, 1)

                def exp(w):
                    if not attn:
                        return
                    act.wait_ge(scores_t, NWIN * t + w + 1)
                    wait(act, lo_done, NWIN * t + w - 1)
                    wait(act, pv_done, NWIN * t + w - 1)
                    act.activation(prob_hi[:, w % 2, :], score[w % 2][:, :], ACT.Exp, scale=exp_scale).then_inc(hi_done, 1)
                    act.activation(prob32[:, w % 2, :], score[w % 2][:, :], ACT.Exp, scale=exp_scale).then_inc(exp_done, 1)

                def scale_projection():
                    act.wait_ge(qk_proj, m + 1)
                    wait(act, lo_ready, m)
                    if pre:
                        act.wait_ge(s_scale, 2)
                    act.activation(qk32[:, :], misc[:, :], ACT.Identity, bias=bias_qk, scale=scale_qk).then_inc(qk_scaled, 1)

                def high_projection():
                    act.wait_ge(k_masked, m + 1)
                    wait(act, stacks_in, 16 * STACK_DMAS * m)
                    act.activation(qk_hi[:, :], qk32[:, :], ACT.Copy).then_inc(hi_ready, 1)

                relu(E - 2, t - 2, par, late)
                if pre:
                    normalize(0)
                    expert_sum(0)
                exp(0)
                exp(1)
                relu(E - 1, t - 2, par, late)
                if prep:
                    act.wait_ge(v_proj, n + 1)
                    wait(act, v_ready, n)
                    act.activation(v32[:, :, :].rearrange("p x d -> p (x d)"), misc[:, 0:NWIN * DK],
                                   ACT.Copy).then_inc(v_copied, 1)
                if proj and not pre:
                    normalize(m)
                if start:
                    expert_sum(2)
                exp(2)
                relu(0)
                if proj:
                    scale_projection()
                exp(3)
                if proj:
                    high_projection()
                if pre:
                    expert_sum(1)
                relu(1)
                relu(2)
                if start:
                    expert_sum(3)
                    expert_sum(4)
                if first:
                    expert_sum(5)
                    expert_sum(6)
                    expert_sum(7)
                relu(3)
                if attn:
                    act.wait_ge(o_t, t + 1)
                    wait(act, wo_done, t)
                    if first:
                        act.wait_ge(small_in, 16 * 8)
                    act.activation(o_gelu[:, :], misc[0:DK, :], ACT.Gelu, bias=bv_c[0:DK, :]).then_inc(gelu_done, 1)
                relu(4)
                relu(5)
                if prep:
                    act.wait_ge(shifts_t, n + 1)
                    if start:
                        act.wait_ge(s_init, 4)
                    act.activation(q_stack[AUX:ROWS_ALL, npar, :, :].rearrange("p g s -> p (g s)"),
                                   pv16[AUX:ROWS_ALL, :], ACT.Copy).then_inc(shift_rows, 1)
                if attn:
                    act.wait_ge(xn2_t, t + 1)
                    wait(act, ffn_done, START + E * (t - 1))
                    act.activation(xt_hi[:, par, :, :].rearrange("p c t -> p (c t)"), misc[:, :],
                                   ACT.Copy).then_inc(xt_hi_ready, 1)

            steps(act, step)

        @block.vector
        def _(dve):
            dve.memset(half_neg[:, :], -0.5).then_inc(s_init, 1)
            dve.memset(q_stack[AUX:P, :, :, :], MASK_Q).then_inc(s_init, 1)
            dve.memset(shifts[:, :, 0:1], MASK_Q).then_inc(s_init, 1)
            dve.memset(v_thirds[:, :, :, :, DH:VC], 0.0).then_inc(s_init, 1)
            dve.wait_ge(s_init, 4)
            dve.memset(v_thirds[:, :, :, 0, DH:VC], 1.0).then_inc(s_init, 1)
            dve.wait_ge(x0_in, 16)
            dve.bn_stats(stats1[:, 0, :], x_all[:, 0, :]).then_inc(s_stat, 1)
            dve.wait_ge(s_stat, 1)
            dve.bn_aggr(mean_var1[:, 0, :], stats1[:, 0, :]).then_inc(s_stat, 1)
            dve.wait_ge(s_stat, 2)
            dve.tensor_scalar(rstd1[:, 0, 0:1], mean_var1[:, 0, 1:2], EPS, None, ALU.add).then_inc(s_var1, 1)
            dve.wait_ge(s_wt, 1)
            dve.tensor_copy(wqk_t[:, :], misc[:, 0:P]).then_inc(s_wt_copied, 1)
            dve.wait_ge(const_in, 16)
            dve.tensor_copy(ident16[:, :], const[:, C_IDENT:C_IDENT + P]).then_inc(s_ident, 1)
            dve.wait_ge(wqk_in, 32)
            dve.tensor_reduce(qk_small[:, 0:1], w_rows[:, 0, :], AX.X, ALU.add, apply_absolute_value=True).then_inc(s_sums, 1)
            dve.wait_ge(small_in, 16 * 8)
            dve.tensor_reduce(qk_small[:, 1:2], bqk, AX.X, ALU.max, apply_absolute_value=True).then_inc(s_sums, 1)
            dve.wait_ge(s_sums, 2)
            dve.tensor_scalar(bound, qk_small[:, 0:1], NORM_BOUND, qk_small[:, 1:2], ALU.mult, ALU.add).then_inc(s_sums, 1)
            dve.wait_ge(s_sums, 3)
            dve.tensor_scalar(qk_small[:, 2:4], const[:, C_SIDE:C_SIDE + 2], bound, QK_FLOOR, ALU.mult, ALU.max).then_inc(s_sums, 1)
            dve.wait_ge(s_bound, 1)
            dve.tensor_scalar(qk_small[:, 4:6].bitcast(I32), qk_small[:, 4:6].bitcast(I32), 0x7F800000, None,
                              ALU.bitwise_and).then_inc(s_sums, 1)
            dve.wait_ge(s_sums, 5)
            dve.reciprocal(qk_small[:, 6:8], qk_small[:, 4:6]).then_inc(s_sums, 1)
            dve.tensor_scalar(exp_scale, qk_small[:, 4:5], qk_small[:, 5:6], float(DH) ** -0.5 / QK_TOP ** 2,
                              ALU.mult, ALU.mult).then_inc(s_sums, 1)
            dve.wait_ge(s_sums, 7)
            dve.tensor_scalar(scale_qk[0:DK, :], qk_small[0:DK, 6:7], QK_TOP, None, ALU.mult).then_inc(s_sums, 1)
            dve.tensor_scalar(scale_qk[DK:2 * DK, :], qk_small[DK:2 * DK, 7:8], QK_TOP, None, ALU.mult).then_inc(s_scale, 1)
            dve.wait_ge(s_sums, 8)
            dve.wait_ge(s_scale, 1)
            dve.tensor_tensor(bias_qk, bqk, scale_qk, ALU.mult).then_inc(s_scale, 1)
            dve.wait_ge(s_tanh, 1)
            dve.tensor_tensor(bo_c, bo_c, tg[:, 0:1], ALU.mult).then_inc(s_wot, 1)
            dve.tensor_copy(wg_thirds[:, :, 0, :], wg_in[:, :, :]).then_inc(s_wg, 1)
            dve.wait_ge(s_wg, 1)
            dve.tensor_tensor(wg_rest[:, :, :], wg_in[:, :, :], wg_thirds[:, :, 0, :], ALU.subtract).then_inc(s_wg, 1)
            dve.wait_ge(s_wg, 2)
            dve.tensor_copy(wg_thirds[:, :, 1, :], wg_rest[:, :, :]).then_inc(s_wg, 1)
            dve.wait_ge(s_wg, 3)
            dve.tensor_tensor(wg_thirds[:, :, 2, :], wg_rest[:, :, :], wg_thirds[:, :, 1, :], ALU.subtract).then_inc(s_wg, 1)

            def statistics(b, e):
                if b == 1:
                    dve.wait_ge(early_in, 16 * (EARLY - 1))
                else:
                    dve.wait_ge(xrest_in, 16 * (B - EARLY))
                for i in range(b, e):
                    dve.bn_stats(stats1[:, i, :], x_all[:, i, :]).then_inc(s_stat, 1)
                for i in range(b, e):
                    dve.wait_ge(s_stat, b + i + 1)
                    dve.bn_aggr(mean_var1[:, i, :], stats1[:, i, :]).then_inc(s_stat, 1)
                dve.wait_ge(s_stat, 2 * e)
                dve.tensor_scalar(rstd1[:, b:e, 0], mean_var1[:, b:e, 1], EPS, None, ALU.add).then_inc(s_var1, 1)

            def expert_scale(e):
                one = slice(e, e + 1)
                dve.wait_ge(s_sum_all, e + 1)
                dve.tensor_scalar(we_pow[:, one], we_bound_all[:, one], 2.0 ** -100, None, ALU.max).then_inc(s_wscale, 1)
                dve.wait_ge(s_wscale, 5 * e + 1)
                dve.tensor_scalar(we_pow[:, one].bitcast(I32), we_pow[:, one].bitcast(I32), 0x7F800000, None,
                                  ALU.bitwise_and).then_inc(s_wscale, 1)
                dve.wait_ge(s_wscale, 5 * e + 2)
                dve.reciprocal(we_scale[:, one], we_pow[:, one]).then_inc(s_wscale, 1)
                dve.tensor_scalar(we_unscale[:, one], we_pow[:, one], 0.5 / WE_TOP, None, ALU.mult).then_inc(s_wscale, 1)
                dve.wait_ge(s_wscale, 5 * e + 3)
                dve.tensor_scalar(we_scale[:, one], we_scale[:, one], WE_TOP, None, ALU.mult).then_inc(s_wscale, 1)

            def expert_low(e):
                dve.wait_ge(s_whi, e + 1)
                dve.scalar_tensor_tensor(we_lo[:, e, :, :].rearrange(flat), we_buf(e), we_scale[:, e:e + 1],
                                         we_hi[:, e, :, :].rearrange(flat), ALU.mult, ALU.subtract).then_inc(s_wlo, 1)
                if e + 1 < E:
                    expert_scale(e + 1)

            def step(t, par, late=False, ffn=False, attn=False, prep=False, proj=False):
                n, npar = t + 1, (par + 1) % 2
                f, fpar = t - 1, (par + 1) % 2
                m = t + 2
                pre, start, first = (isinstance(t, int) and t == at for at in (-2, -1, 0))

                def add_bias(e, fb=f, on=ffn):
                    if not on:
                        return
                    dve.wait_ge(ffn_done, START + E * fb + e + 1)
                    if isinstance(t, int) and t == 1:
                        dve.wait_ge(s_ebias, e + 1)
                    dve.tensor_tensor(ffn_bank[e % 2][:, :], ffn_bank[e % 2][:, :], expert_bias[:, e, :],
                                      ALU.add).then_inc(biased, 1)

                def shift_of_norm(b, e):
                    dve.scalar_tensor_tensor(shift1[:, b:e, 0], mean_var1[:, b:e, 0], -1.0, rstd1[:, b:e, 1],
                                             ALU.mult, ALU.mult).then_inc(s_shift1, 1)

                def low_half(w):
                    if not attn:
                        return
                    dve.wait_ge(exp_done, NWIN * t + w + 1)
                    wait(dve, pv_done, NWIN * t + w - 1)
                    dve.tensor_tensor(prob_lo[:, w % 2, :], prob32[:, w % 2, :], prob_hi[:, w % 2, :],
                                      ALU.subtract).then_inc(lo_done, 1)

                def maxima(w):
                    if not prep:
                        return
                    dve.wait_ge(scores, NWIN * n + w + 1)
                    dve.tensor_reduce(row_max[:, :, w, :], score[w % 2][:, :].rearrange("p (g h j) -> p g h j", g=NG, h=HG),
                                      AX.X, ALU.max).then_inc(max_done, 1)

                def add_windows(half):
                    if not attn:
                        return
                    dve.wait_ge(pv_done, NWIN * t + 2 * half + 2)
                    n_in = 2 * H
                    dve.tensor_reduce(o_sum[:, half * n_in:(half + 1) * n_in, :],
                                      pv[:, 0:n_in * THIRDS * VC].rearrange("p (x q c) -> p x c q", q=THIRDS, c=VC),
                                      AX.X, ALU.add).then_inc(pv_read, 1)

                def mask_keys():
                    dve.wait_ge(qk_scaled, m + 1)
                    dve.scalar_tensor_tensor(qk32[DK:2 * DK, :], mask_all[DK:2 * DK, m, :], 0.0, qk32[DK:2 * DK, :],
                                             ALU.is_gt, ALU.mult).then_inc(k_masked, 1)

                def low_projection():
                    dve.wait_ge(hi_ready, m + 1)
                    wait(dve, stacks_in, 16 * STACK_DMAS * m)
                    dve.tensor_tensor(qk_lo[:, :], qk32[:, :], qk_hi[:, :], ALU.subtract).then_inc(lo_ready, 1)

                def row_of_mask():
                    if isinstance(t, int) and m in (0, EARLY):
                        dve.wait_ge(mask_early_in if m == 0 else mask_in, 16)
                    wait(dve, k_ready, m)
                    dve.tensor_scalar(k_rows[AUX:P, :, :], mask_all[AUX:P, m, :].unsqueeze(1).broadcast_to([P - AUX, NG, S]),
                                      0.0, -AUX_K, ALU.is_le, ALU.mult).then_inc(mask_row, 1)

                if pre:
                    dve.wait_ge(s_rstd1, 1)
                    shift_of_norm(0, 1)
                if late:
                    add_bias(E - 2, t - 2, late)
                if ffn:
                    dve.wait_ge(logits, f + 1)
                    dve.tensor_reduce(logit[:, 0, :], misc[:, 0:THIRDS * E].rearrange("p (q e) -> p e q", q=THIRDS),
                                      AX.X, ALU.add).then_inc(logits_read, 1)
                    dve.wait_ge(logits_read, f + 1)
                    dve.tensor_tensor(logit[:, 1, :], logit[:, 0, :], bg_b[:, :], ALU.add).then_inc(s_gate, 1)
                    dve.wait_ge(s_gate, 7 * f + 1)
                    other = logit[:, 1, :].unsqueeze(1).broadcast_to([P, E, E])
                    own = logit[:, 1, :].unsqueeze(2).broadcast_to([P, E, E])
                    earlier = const[:, C_EARLIER:C_EARLIER + E * E].rearrange("p (e j) -> p e j", e=E)
                    dve.tensor_tensor(pairs[:, 0, :, :], other, own, ALU.is_gt).then_inc(s_gate, 1)
                    dve.tensor_tensor(pairs[:, 1, :, :], other, own, ALU.is_equal).then_inc(s_gate, 1)
                    dve.wait_ge(s_gate, 7 * f + 3)
                    dve.tensor_tensor(pairs[:, 1, :, :], pairs[:, 1, :, :], earlier, ALU.mult).then_inc(s_gate, 1)
                    dve.tensor_reduce(rank[:, 0, :], pairs[:, 0, :, :], AX.X, ALU.add).then_inc(s_gate, 1)
                    dve.wait_ge(s_gate, 7 * f + 4)
                    dve.tensor_reduce(rank[:, 1, :], pairs[:, 1, :, :], AX.X, ALU.add).then_inc(s_gate, 1)
                    dve.wait_ge(s_gate, 7 * f + 6)
                    dve.tensor_tensor(rank[:, 0, :], rank[:, 0, :], rank[:, 1, :], ALU.add).then_inc(s_gate, 1)
                    dve.wait_ge(s_gate, 7 * f + 7)
                    wait(dve, relu_done, START + E * (f - 1))
                    dve.scalar_tensor_tensor(gate[:, fpar, :], rank[:, 0, :], 1.5, we_unscale[:, :], ALU.is_lt,
                                             ALU.mult).then_inc(gates_ready, 1)
                if prep:
                    dve.wait_ge(stacks_in, 16 * STACK_DMAS * (n + 1))
                    dve.wait_ge(mask_row, n + 1)
                    wait(dve, scores_t, NWIN * (n - 1))
                    for h in range(HG):
                        mm = dve.tensor_scalar(k_stack[:, npar, :, h, :], k_rows[:, :, :], const[:, C_HEAD + h:C_HEAD + h + 1],
                                               const[:, C_ONE + h:C_ONE + h + 1], ALU.mult, ALU.add)
                    mm.then_inc(k_ready, 1)
                low_half(0)
                if late:
                    add_bias(E - 1, t - 2, late)
                low_half(1)
                if first:
                    expert_low(2)
                add_bias(0)
                if proj:
                    row_of_mask()
                low_half(2)
                if proj:
                    mask_keys()
                if attn:
                    add_windows(0)
                add_bias(1)
                if proj:
                    low_projection()
                if pre:
                    statistics(1, EARLY)
                    expert_scale(0)
                    expert_low(0)
                    dve.wait_ge(s_rstd1, 2)
                    shift_of_norm(1, EARLY)
                    expert_low(1)
                low_half(3)
                if first:
                    expert_low(3)
                maxima(0)
                add_bias(2)
                maxima(1)
                if first:
                    expert_low(4)
                if attn:
                    add_windows(1)
                    dve.wait_ge(pv_read, 2 * t + 2)
                    dve.reciprocal(o_den[:, :], o_sum[:, :, DH]).then_inc(den_ready, 1)
                    dve.wait_ge(den_ready, t + 1)
                    wait(dve, o_t, t)
                    dve.tensor_tensor(o_norm[:, :, :], o_sum[:, :, 0:DH],
                                      o_den[:, :].unsqueeze(2).broadcast_to([P, NWIN * H, DH]), ALU.mult).then_inc(o_ready, 1)
                if late:
                    dve.wait_ge(summed, START + (E - 1) * (t - 1))
                    dve.scalar_tensor_tensor(total[:, par, :], total[:, par, :], tg[:, 1:2], x_all[:, t - 2, :],
                                             ALU.mult, ALU.add).then_inc(out_ready, 1)
                add_bias(3)
                maxima(2)
                if first:
                    expert_low(5)
                maxima(3)
                if prep:
                    dve.wait_ge(max_done, NWIN * (n + 1))
                    wait(dve, shifts_t, n)
                    rows = row_max[:, :, :, :].rearrange("p g w h -> p (g w) h")
                    dve.tensor_scalar(shifts[:, :, 1:1 + HG], rows, -1.0 / AUX_K, None, ALU.mult).then_inc(max_hi, 1)
                    dve.wait_ge(max_hi, n + 1)
                    dve.scalar_tensor_tensor(shifts[:, :, 1 + HG:1 + 2 * HG], rows, -1.0 / AUX_K, shifts[:, :, 1:1 + HG],
                                             ALU.mult, ALU.subtract).then_inc(shifts_ready, 1)
                if first:
                    expert_low(6)
                add_bias(4)
                if attn:
                    dve.wait_ge(wo_done, t + 1)
                    if first:
                        dve.wait_ge(s_wot, 1)
                    dve.scalar_tensor_tensor(attn_out[:, :], misc[:, :], bo_c, mask_all[:, t, :], ALU.add,
                                             ALU.mult).then_inc(attn_masked, 1)
                    dve.wait_ge(attn_masked, t + 1)
                    dve.tensor_tensor(x_all[:, t, :], x_all[:, t, :], attn_out[:, :], ALU.add).then_inc(x1_ready, 1)
                    wait_alone(dve, (x1_ready, t + 1))
                    dve.bn_stats(stats2[:, :], x_all[:, t, :]).then_inc(s_stat2, 1)
                    wait_alone(dve, (s_stat2, 2 * t + 1))
                    dve.bn_aggr(mean_var2[:, 0:2], stats2[:, :]).then_inc(s_stat2, 1)
                    dve.wait_ge(s_stat2, 2 * t + 2)
                    dve.tensor_scalar(mean_var2[:, 2:3], mean_var2[:, 1:2], EPS, None, ALU.add).then_inc(s_var2, 1)
                    dve.wait_ge(s_rstd2, t + 1)
                    wait(dve, xn2_t, t)
                    dve.tensor_scalar(xn2[:, :], x_all[:, t, :], mean_var2[:, 0:1], mean_var2[:, 3:4],
                                      ALU.subtract, ALU.mult).then_inc(xn2_ready, 1)
                add_bias(5)
                if first:
                    expert_low(7)
                    statistics(EARLY, B)
                    dve.wait_ge(s_rstd1, 3)
                    shift_of_norm(EARLY, B)
                if attn:
                    dve.wait_ge(xt_hi_ready, t + 1)
                    dve.tensor_tensor(xt_lo[:, par, :, :].rearrange("p c t -> p (c t)"), misc[:, :],
                                      xt_hi[:, par, :, :].rearrange("p c t -> p (c t)"), ALU.subtract).then_inc(xt_lo_ready, 1)

            steps(dve, step)

        @block.gpsimd
        def _(pool):
            def load_expert(e):
                pool.dma_start(we_buf(e).rearrange("p (k s) -> p k s", k=KC),
                               w_e[e].rearrange("(k p) s -> p k s", p=P)).then_inc(we_loaded[e % WE_BUFS], 16)

            def expert_bound(e):
                pool.wait_ge(s_sum, e + 1)
                pool.partition_all_reduce(we_bound_all[:, e:e + 1], we_bound[:, e:e + 1], P, MAXIMUM).then_inc(s_sum_all, 1)

            def expert_hi(e):
                expert_bound(e)
                pool.wait_ge(s_wscale, 5 * e + 5)
                pool.tensor_scalar(we_hi[:, e, :, :].rearrange(flat), we_buf(e),
                                   we_scale[:, e:e + 1], 1.0, ALU.mult, ALU.mult).then_inc(s_whi, 1)
                if 1 <= e < E - WE_BUFS + 1:
                    pool.wait_ge(s_wlo, e)
                    load_expert(e + WE_BUFS - 1)

            def bias_of_experts():
                pool.wait_ge(bias_in, 16)
                for e in range(E):
                    pool.tensor_scalar(expert_bias[:, e, :], expert_bias[:, e, :], we_scale[:, e:e + 1], 1.0,
                                       ALU.mult, ALU.mult).then_inc(s_ebias, 1)

            pool.sem_inc(summed, START)
            pool.wait_ge(s_init, 1)

            def rstd_of(b, e):
                pool.wait_ge(s_var1, part_of_batch(b))
                pool.tensor_tensor(rstd1[:, b:e, 1], rstd1[:, b:e, 0], half_neg[:, :].broadcast_to([P, e - b]),
                                   ALU.pow).then_inc(s_rstd1, 1)

            rstd_of(0, 1)
            pool.wait_ge(s_sums, 4)
            pool.partition_all_reduce(qk_small[:, 4:6], qk_small[:, 2:4], P, MAXIMUM).then_inc(s_bound, 1)
            pool.wait_ge(wvo_in, 32)
            for e in range(WE_BUFS):
                load_expert(e)

            def step(t, par, late=False, ffn=False, attn=False, prep=False, proj=False):
                n, npar = t + 1, (par + 1) % 2
                f, fpar = t - 1, (par + 1) % 2
                pre, start, first = (isinstance(t, int) and t == at for at in (-2, -1, 0))

                def accumulate(e, fb=f, half=fpar, on=ffn):
                    if not on or e == 0:
                        return
                    pool.wait_ge(relu_done, START + E * fb + e + 1)
                    pool.wait_ge(summed, START + (E - 1) * fb + e - 1)
                    pool.tensor_tensor(total[:, half, :], total[:, half, :], expert_out[:, e % 2, :],
                                       ALU.add).then_inc(summed, 1)

                if late:
                    accumulate(E - 2, t - 2, par, late)
                    accumulate(E - 1, t - 2, par, late)
                accumulate(0)
                if pre:
                    expert_hi(0)
                    rstd_of(1, EARLY)
                    expert_hi(1)
                if first:
                    expert_hi(3)
                if prep:
                    thirds = v_thirds[:, npar, :, :, :]
                    wait_alone(pool, (v_copied, n + 1), (pv_done, NWIN * (n - 1)))
                    if isinstance(n, int) and n == 0:
                        pool.wait_ge(s_init, 5)
                    pool.tensor_copy(thirds[:, :, 0, 0:DH], v32[:, :, :]).then_inc(v_step, 1)
                    pool.wait_ge(v_step, 4 * n + 1)
                    pool.tensor_tensor(v32[:, :, :], v32[:, :, :], thirds[:, :, 0, 0:DH], ALU.subtract).then_inc(v_step, 1)
                    wait_alone(pool, (v_step, 4 * n + 2))
                    pool.tensor_copy(thirds[:, :, 1, 0:DH], v32[:, :, :]).then_inc(v_step, 1)
                    pool.wait_ge(v_step, 4 * n + 3)
                    pool.tensor_tensor(v32[:, :, :], v32[:, :, :], thirds[:, :, 1, 0:DH], ALU.subtract).then_inc(v_step, 1)
                    wait_alone(pool, (v_step, 4 * n + 4))
                    pool.tensor_copy(thirds[:, :, 2, 0:DH], v32[:, :, :]).then_inc(v_ready, 1)
                if start:
                    expert_hi(2)
                if first:
                    for e in range(4, 8):
                        expert_hi(e)
                accumulate(1)
                accumulate(2)
                accumulate(3)
                if attn:
                    pool.wait_ge(s_var2, t + 1)
                    pool.tensor_tensor(mean_var2[:, 3:4], mean_var2[:, 2:3], half_neg[:, :], ALU.pow).then_inc(s_rstd2, 1)
                accumulate(4)
                accumulate(5)
                if first:
                    rstd_of(EARLY, B)
                    bias_of_experts()

            steps(pool, step)


_INS = ["x", "ctx_4096", "mask_Bx1x4096_ff1", "g_xattn", "g_ffn", "L0_xattn_Wq", "L0_xattn_bq", "L0_xattn_Wk",
        "L0_xattn_bk", "L0_xattn_Wv", "L0_xattn_bv", "L0_xattn_Wo", "L0_xattn_bo", "L0_ffn_W_gate",
        "L0_ffn_b_gate", "L0_ffn_W_e", "L0_ffn_b_e"]


def kernel(**inputs):
    import numpy as np
    import concourse.bacc as bacc
    from concourse.bass_utils import run_bass_kernel_spmd as run

    nc = bacc.Bacc("TRN2", target_bir_lowering=False, num_devices=1)
    arrays, args = {}, []
    for name in _INS:
        a = np.ascontiguousarray(inputs[name])
        arrays[f"in_{name}"] = a
        args.append(nc.dram_tensor(f"in_{name}", a.shape, mybir.dt.from_np(a.dtype), kind="ExternalInput").ap())
    arrays["in_constants"] = shape_constants()
    args.append(nc.dram_tensor("in_constants", (P, C_END), F32, kind="ExternalInput").ap())
    args.append(nc.dram_tensor("out_0", (B, D, S), F32, kind="ExternalOutput").ap())
    build(nc, *args)
    return run(nc, [arrays], core_ids=[0]).results[0]["out_0"]
```

```python
from contextlib import ExitStack

import concourse.bass as bass
from concourse import mybir

F32 = mybir.dt.float32
F16 = mybir.dt.float16
BF16 = mybir.dt.bfloat16
I32 = mybir.dt.int32
ALU = mybir.AluOpType
ACT = mybir.ActivationFunctionType
AX = mybir.AxisListType

START = 1
MAXIMUM = bass.bass_isa.ReduceOp.max

P = 128
B, D, S = 8, 128, 512
W = 128
NWIN = S // W
H, DH = 8, 8
DK = H * DH
NG = 2
HG = H // NG
QUAD = HG * DH
E = 8
KC = S // P
EPS = 1e-5
NORM_BOUND = 22.7
QK_FLOOR = 8.0
QK_TOP = 2.0 ** 11
WE_TOP = 2.0 ** 14
AUX = 3 * QUAD
ROWS_MASK = AUX + 1
ROWS_ALL = AUX + 1 + 2 * HG
MASK_Q = 2.0 ** 15
AUX_K = 2.0 ** 14
THIRDS = 3
EARLY = 4
VC = DH + 1
WE_BUFS = 5
STACK_DMAS = 12

C_IDENT = 0
C_HEAD = C_IDENT + P
C_ONE = C_HEAD + HG
C_EARLIER = C_ONE + HG
C_SIDE = C_EARLIER + E * E
C_END = C_SIDE + 2


def shape_constants():
    import numpy as np

    c = np.zeros((P, C_END), np.float32)
    c[:, C_IDENT:C_IDENT + P] = np.eye(P)
    for h in range(HG):
        for third in range(3):
            at = third * QUAD + h * DH
            c[at:at + DH, C_HEAD + h] = 1
        c[AUX, C_HEAD + h] = 1
        c[AUX + 1 + h, C_ONE + h] = AUX_K
        c[AUX + 1 + HG + h, C_ONE + h] = AUX_K
    for e in range(E):
        for j in range(e):
            c[:, C_EARLIER + e * E + j] = 1
    c[0:DK, C_SIDE] = 1
    c[DK:2 * DK, C_SIDE + 1] = 1
    return c


def build(nc, x, ctx_in, mask, g_xattn, g_ffn, wq, bq, wk, bk, wv, bv, wo, bo,
          w_gate, b_gate, w_e, b_e, consts, out):
    stack = ExitStack()
    with stack:
        def sb(name, shape, dt=F32):
            return stack.enter_context(nc.sbuf_tensor(name, shape, dt))

        def pb(name, shape, dt=F32):
            return stack.enter_context(nc.psum_tensor(name, shape, dt))

        def sem(name):
            return stack.enter_context(nc.semaphore(name))

        x_all = sb("x_all", [P, B, S])
        mask_all = sb("mask_all", [P, B, S])
        expert_bias = sb("expert_bias", [P, E, S])
        we_in = sb("we_in", [P, 2, KC, S])
        total = sb("total", [P, 2, S])
        expert_out = sb("expert_out", [P, 2, S])
        we_hi = sb("we_hi", [P, E, KC, S], F16)
        we_lo = sb("we_lo", [P, E, KC, S], F16)
        ctx_sb = sb("ctx_sb", [P, 2, S])
        const = sb("const", [P, C_END])
        w_rows = sb("w_rows", [P, 3, P])
        wqk_t = sb("wqk_t", [P, P])
        wv_t = sb("wv_t", [P, DK])
        wo_t = sb("wo_t", [DK, P])
        bv_c = sb("bv_c", [P, 1])
        wg_in = sb("wg_in", [P, KC, E])
        wg_rest = sb("wg_rest", [P, KC, E])
        wg_thirds = sb("wg_thirds", [P, KC, THIRDS, E], BF16)
        ident16 = sb("ident16", [P, P], F16)
        col = sb("col", [P, 10])
        bqk, bo_c, g2, tg, scale_qk = col[:, 0:1], col[:, 1:2], col[:, 2:4], col[:, 4:6], col[:, 6:7]
        bias_qk, exp_scale, bound = col[:, 7:8], col[:, 8:9], col[:, 9:10]
        half_neg = sb("half_neg", [P, 1])
        table = sb("table", [P, 3])
        bg_b = sb("bg_b", [P, E])
        qk_small = sb("qk_small", [P, 8])
        we_bound = sb("we_bound", [P, E])
        we_bound_all = sb("we_bound_all", [P, E])
        we_pow = sb("we_pow", [P, E])
        we_scale = sb("we_scale", [P, E])
        we_unscale = sb("we_unscale", [P, E])

        stats1 = sb("stats1", [P, B, 6])
        mean_var1 = sb("mean_var1", [P, B, 2])
        rstd1 = sb("rstd1", [P, B, 2])
        shift1 = sb("shift1", [P, B, 1])
        xn = sb("xn", [P, S])
        qk32 = sb("qk32", [P, S])
        qk_hi = sb("qk_hi", [P, S], F16)
        qk_lo = sb("qk_lo", [P, S], F16)
        q_stack = sb("q_stack", [P, 2, NG, S], F16)
        k_rows = sb("k_rows", [P, NG, S], F16)
        k_stack = sb("k_stack", [P, 2, NG, HG, S], F16)
        row_max = sb("row_max", [P, NG, NWIN, HG])
        shifts = sb("shifts", [P, NG * NWIN, 1 + 2 * HG], F16)
        prob32 = sb("prob32", [P, 2, H * W])
        prob_hi = sb("prob_hi", [P, 2, H * W], F16)
        prob_lo = sb("prob_lo", [P, 2, H * W], F16)
        v32 = sb("v32", [P, NWIN * H, DH])
        v_thirds = sb("v_thirds", [P, 2, NWIN * H, THIRDS, VC], BF16)
        o_sum = sb("o_sum", [P, NWIN * H, VC])
        o_den = sb("o_den", [P, NWIN * H])
        o_norm = sb("o_norm", [P, NWIN * H, DH])
        o_gelu = sb("o_gelu", [DK, S])
        attn_out = sb("attn_out", [P, S])

        stats2 = sb("stats2", [P, 6])
        mean_var2 = sb("mean_var2", [P, 4])
        xn2 = sb("xn2", [P, S])
        xt_hi = sb("xt_hi", [P, 2, KC, P], F16)
        xt_lo = sb("xt_lo", [P, 2, KC, P], F16)
        logit = sb("logit", [P, 2, E])
        pairs = sb("pairs", [P, 2, E, E])
        rank = sb("rank", [P, 2, E])
        gate = sb("gate", [P, 2, E])

        score = [pb(f"score{i}", [P, H * W]) for i in range(2)]
        ffn_bank = [pb(f"ffn{i}", [P, S]) for i in range(2)]
        pv = pb("pv", [P, S])
        misc = pb("misc", [P, S])
        pv16 = pv[:, :].bitcast(F16)

        const_in, wqk_in, x0_in, x1_in, xrest_in, mask_early_in, mask_in = map(
            sem, ("const_in", "wqk_in", "x0_in", "x1_in", "xrest_in", "mask_early_in", "mask_in"))
        wvo_in, bqk_in, small_in, bias_in = map(sem, ("wvo_in", "bqk_in", "small_in", "bias_in"))
        ctx_loaded = [sem(f"ctx_loaded{i}") for i in range(2)]
        we_loaded = [sem(f"we_loaded{i}") for i in range(WE_BUFS)]
        s_wt, s_wqk_copied, s_wvo_copied, s_sums, s_bound, s_scale, s_tanh = map(
            sem, ("s_wt", "s_wqk_copied", "s_wvo_copied", "s_sums", "s_bound", "s_scale", "s_tanh"))
        s_wot, s_wg, s_init, s_sum, s_sum_all, s_wscale, s_whi, s_ebias = map(
            sem, ("s_wot", "s_wg", "s_init", "s_sum", "s_sum_all", "s_wscale", "s_whi", "s_ebias"))
        s_wscaled, pool_low, dve_low = map(sem, ("s_wscaled", "pool_low", "dve_low"))
        s_stat, s_var1, s_rstd1, s_shift1 = map(sem, ("s_stat", "s_var1", "s_rstd1", "s_shift1"))
        xn_ready, qk_proj, qk_scaled, k_masked, hi_ready, lo_ready, stacks_in = map(
            sem, ("xn_ready", "qk_proj", "qk_scaled", "k_masked", "hi_ready", "lo_ready", "stacks_in"))
        mask_row, k_ready, v_proj, v_copied, v_step, v_ready = map(
            sem, ("mask_row", "k_ready", "v_proj", "v_copied", "v_step", "v_ready"))
        scores, max_done, max_hi, shifts_ready, shifts_t, shift_rows = map(
            sem, ("scores", "max_done", "max_hi", "shifts_ready", "shifts_t", "shift_rows"))
        scores_t, exp_done, hi_done, lo_done, pv_done = map(
            sem, ("scores_t", "exp_done", "hi_done", "lo_done", "pv_done"))
        pv_read, den_ready, o_ready, o_t, gelu_done, wo_done, attn_masked, x1_ready = map(
            sem, ("pv_read", "den_ready", "o_ready", "o_t", "gelu_done", "wo_done", "attn_masked", "x1_ready"))
        s_stat2, s_var2, s_rstd2, xn2_ready, xn2_t, xt_hi_ready, xt_lo_ready = map(
            sem, ("s_stat2", "s_var2", "s_rstd2", "xn2_ready", "xn2_t", "xt_hi_ready", "xt_lo_ready"))
        logits, logits_read, s_gate, gates_ready = map(sem, ("logits", "logits_read", "s_gate", "gates_ready"))
        ffn_done, biased, relu_done, summed, out_ready = map(
            sem, ("ffn_done", "biased", "relu_done", "summed", "out_ready"))
        out_done = [sem(f"out_done{i}") for i in range(2)]

        flat = "p k s -> p (k s)"

        all_flat = "p e k s -> p (e k s)"
        we_bufs = (we_in[:, 0, :, :].rearrange(flat), we_in[:, 1, :, :].rearrange(flat),
                   mask_all[:, EARLY:B, :].rearrange(flat),
                   we_hi[:, E - 2:E, :, :].rearrange(all_flat).bitcast(F32),
                   we_lo[:, E - 2:E, :, :].rearrange(all_flat).bitcast(F32))

        def we_buf(e):
            return we_bufs[e % WE_BUFS]

        low_of_pool = (1, 5, E - 1)

        def wait_low(eng, e):
            if e in low_of_pool:
                eng.wait_ge(pool_low, low_of_pool.index(e) + 1)
            else:
                eng.wait_ge(dve_low, e + 1 - sum(i < e for i in low_of_pool))

        block = stack.enter_context(nc.Block())

        def wait(eng, semaphore, value):
            if isinstance(value, int) and value <= 0:
                return
            eng.wait_ge(semaphore, value)

        def wait_alone(eng, *waits):
            for _, value in waits:
                if not isinstance(value, int):
                    eng.lower_val(value)
            eng.wait_ge(const_in, 16)
            for semaphore, value in waits:
                wait(eng, semaphore, value)

        def steps(eng, step):
            step(-2, 0, proj=True)
            step(-1, 1, prep=True, proj=True)
            step(0, 0, attn=True, prep=True, proj=True)
            step(1, 1, ffn=True, attn=True, prep=True, proj=True)
            with eng.Fori(1, B // 2 - 1) as i:
                step(2 * i, 0, late=True, ffn=True, attn=True, prep=True, proj=True)
                step(2 * i + 1, 1, late=True, ffn=True, attn=True, prep=True, proj=True)
            step(B - 2, 0, late=True, ffn=True, attn=True, prep=True)
            step(B - 1, 1, late=True, ffn=True, attn=True)
            step(B, 0, late=True, ffn=True)
            step(B + 1, 1, late=True)

        @block.sync
        def _(sp):
            for half in out_done:
                sp.sem_inc(half, 16 * START)

            def column(to, vector, done=small_in):
                sp.dma_start(to, vector.rearrange("(e o) -> e o", o=1)).then_inc(done, 16)

            def on_all(to, vector):
                sp.dma_start(to, vector.rearrange("(o e) -> o e", o=1).broadcast_to(to.shape)).then_inc(small_in, 16)

            sp.dma_start(x_all[:, 0, :], x[0]).then_inc(x0_in, 16)
            sp.dma_start(w_rows[0:DK, 0, :], wq).then_inc(wqk_in, 16)
            sp.dma_start(w_rows[DK:2 * DK, 0, :], wk).then_inc(wqk_in, 16)
            sp.dma_start(const[:, :], consts).then_inc(const_in, 16)
            column(bqk[0:DK, :], bq, bqk_in)
            column(bqk[DK:2 * DK, :], bk, bqk_in)
            sp.dma_start(mask_all[:, 0:EARLY, :],
                         mask[0:EARLY].rearrange("b o s -> o b s").broadcast_to([P, EARLY, S])).then_inc(mask_early_in, 16)
            sp.dma_start(x_all[:, 1, :], x[1]).then_inc(x1_in, 16)
            sp.dma_start(w_rows[0:DK, 1, :], wv).then_inc(wvo_in, 16)
            sp.dma_start(w_rows[:, 2, 0:DK], wo).then_inc(wvo_in, 16)
            for b in range(2):
                sp.dma_start(ctx_sb[:, b, :], ctx_in[b]).then_inc(ctx_loaded[b], 16)
            column(bo_c, bo)
            column(bv_c[0:DK, :], bv)
            on_all(g2[:, 0:1], g_xattn)
            on_all(g2[:, 1:2], g_ffn)
            on_all(bg_b[:, :], b_gate)
            sp.dma_start(wg_in[:, :, :], w_gate.rearrange("(k p) e -> p k e", p=P)).then_inc(small_in, 16)
            sp.dma_start(x_all[:, 2:B, :], x[2:B].rearrange("b p s -> p b s")).then_inc(xrest_in, 16)

            def step(t, par, late=False, ffn=False, attn=False, prep=False, proj=False):
                if proj and not (isinstance(t, int) and t < 0):
                    wait_alone(sp, (v_proj, t + 1))
                    sp.dma_start(ctx_sb[:, par, :], ctx_in[t + 2]).then_inc(ctx_loaded[par], 16)
                if isinstance(t, int) and t == 0:
                    sp.dma_start(expert_bias[:, :, :],
                                 b_e.rearrange("(o e) s -> o e s", o=1).broadcast_to([P, E, S])).then_inc(bias_in, 16)
                if proj:
                    m = t + 2
                    wait_alone(sp, (hi_ready, m + 1), (scores_t, NWIN * (t + 1)), (k_ready, m))
                    for third in range(THIRDS):
                        if third == 1:
                            wait_alone(sp, (lo_ready, m + 1))
                        for g in range(NG):
                            q_at, k_at = QUAD * g, DK + QUAD * g
                            rows = slice(QUAD * third, QUAD * (third + 1))
                            sp.dma_start(k_rows[rows, g, :],
                                         (qk_hi, qk_hi, qk_lo)[third][k_at:k_at + QUAD, :]).then_inc(stacks_in, 16)
                            sp.dma_start(q_stack[rows, par, g, :],
                                         (qk_hi, qk_lo, qk_hi)[third][q_at:q_at + QUAD, :]).then_inc(stacks_in, 16)
                if isinstance(t, int) and t == 1:
                    wait_low(sp, E - 1)
                    sp.dma_start(mask_all[:, EARLY:B, :],
                                 mask[EARLY:B].rearrange("b o s -> o b s").broadcast_to([P, B - EARLY, S])
                                 ).then_inc(mask_in, 16)
                if late:
                    wait_alone(sp, (out_ready, t - 1))
                    sp.dma_start(out[t - 2], total[:, par, :]).then_inc(out_done[par], 16)

            steps(sp, step)
            for half in out_done:
                sp.wait_ge(half, 16 * START + 16 * B // 2)

        @block.tensor
        def _(pe):
            pe.sem_inc(ffn_done, START)
            pe.wait_ge(const_in, 16)
            pe.wait_ge(wqk_in, 32)
            ident32 = const[:, C_IDENT:C_IDENT + P]
            pe.transpose(misc[:, 0:P], w_rows[:, 0, :], ident32).then_inc(s_wt, 1)
            pe.wait_ge(s_wqk_copied, 1)

            def score_maxima(n, np_, w):
                slot = score[w % 2]
                if w < 2:
                    wait(pe, exp_done, NWIN * (n - 1) + w + 3)
                else:
                    wait(pe, max_done, NWIN * n + w - 1)
                if w == 0:
                    pe.wait_ge(k_ready, n + 1)
                for g in range(NG):
                    mm = pe.matmul(slot[:, g * HG * W:(g + 1) * HG * W].rearrange("p (h j) -> p h j", h=HG),
                                   q_stack[0:ROWS_MASK, np_, g, w * W:(w + 1) * W],
                                   k_stack[0:ROWS_MASK, np_, g, :, w * W:(w + 1) * W], start=True, stop=True)
                mm.then_inc(scores, 1)

            def score_shifted(t, par, w):
                slot = score[w % 2]
                if w < 2:
                    wait(pe, max_done, NWIN * t + w + 3)
                else:
                    wait(pe, exp_done, NWIN * t + w - 1)
                if w == 0:
                    pe.wait_ge(shift_rows, t + 1)
                for h in range(H):
                    g, hg = h // HG, h % HG
                    mm = pe.matmul(slot[:, h * W:(h + 1) * W],
                                   k_stack[0:ROWS_ALL, par, g, hg, w * W:(w + 1) * W],
                                   q_stack[0:ROWS_ALL, par, g, w * W:(w + 1) * W], start=True, stop=True)
                mm.then_inc(scores_t, 1)

            def weigh_values(t, par, w):
                pe.wait_ge(lo_done, NWIN * t + w + 1)
                if w == 0:
                    pe.wait_ge(v_ready, t + 1)
                if w % 2 == 0:
                    wait(pe, pv_read, 2 * t + w // 2)
                for h in range(H):
                    at = ((w % 2) * H + h) * THIRDS * VC
                    v = v_thirds[:, par, w * H + h, :, :].rearrange("p q c -> p (q c)")
                    for part, half in enumerate((prob_hi, prob_lo)):
                        mm = pe.matmul(pv[:, at:at + THIRDS * VC], half[:, w % 2, h * W:(h + 1) * W], v,
                                       start=(part == 0), stop=(part == 1))
                mm.then_inc(pv_done, 1)

            def expert(f, fpar, e, split, chunks=range(KC)):
                if chunks[0] == 0:
                    if e == 0:
                        pe.wait_ge(xt_hi_ready, f + 1)
                        pe.wait_ge(xt_lo_ready, f + 1)
                    if split:
                        wait_low(pe, e)
                    wait(pe, relu_done, START + E * f + e - 1)
                for c in chunks:
                    for i, (xs, ws) in enumerate(((xt_hi, we_hi), (xt_hi, we_lo), (xt_lo, we_hi))):
                        mm = pe.matmul(ffn_bank[e % 2][:, :], xs[:, fpar, c, :], ws[:, e, c, :],
                                       start=(c == 0 and i == 0), stop=(c == KC - 1 and i == 2))
                if chunks[-1] == KC - 1:
                    mm.then_inc(ffn_done, 1)

            def step(t, par, late=False, ffn=False, attn=False, prep=False, proj=False):
                n, npar = t + 1, (par + 1) % 2
                f, fpar = t - 1, (par + 1) % 2
                first, second = (isinstance(t, int) and t == at for at in (0, 1))
                split = isinstance(t, int) and t < 3

                def ex(e, chunks=range(KC)):
                    if ffn:
                        expert(f, fpar, e, split, chunks)

                def project():
                    if not proj:
                        return
                    pe.wait_ge(xn_ready, t + 3)
                    wait(pe, v_copied, n + 1)
                    pe.matmul(misc[:, :], wqk_t[:, :], xn[:, :], start=True, stop=True).then_inc(qk_proj, 1)

                def ex_late(e):
                    if late:
                        expert(t - 2, par, e, True)

                ex_late(E - 2)
                if ffn:
                    pe.wait_ge(xt_hi_ready, f + 1)
                    pe.wait_ge(xt_lo_ready, f + 1)
                    for c in range(KC):
                        for i, xs in enumerate((xt_hi, xt_lo)):
                            mm = pe.matmul(misc[:, 0:THIRDS * E], xs[:, fpar, c, :],
                                           wg_thirds[:, c, :, :].rearrange("p q e -> p (q e)"),
                                           start=(c == 0 and i == 0), stop=(c == KC - 1 and i == 1))
                    mm.then_inc(logits, 1)
                if attn:
                    score_shifted(t, par, 0)
                    score_shifted(t, par, 1)
                ex_late(E - 1)
                if second:
                    ex(0)
                if prep:
                    if isinstance(t, int):
                        pe.wait_ge(ctx_loaded[npar], 16 * (n // 2 + 1))
                    else:
                        pe.wait_ge(ctx_loaded[npar], (n - npar) * 8 + 16)
                    pe.wait_ge(qk_scaled, n + 1)
                    if ffn:
                        pe.wait_ge(logits_read, t)
                    for w in range(NWIN):
                        mm = pe.matmul(misc[:, w * DK:(w + 1) * DK], ctx_sb[:, npar, w * W:(w + 1) * W],
                                       wv_t[:, :], start=True, stop=True)
                    mm.then_inc(v_proj, 1)
                if attn:
                    weigh_values(t, par, 0)
                    score_shifted(t, par, 2)
                if not second:
                    ex(0)
                if attn:
                    weigh_values(t, par, 1)
                    score_shifted(t, par, 3)
                if not first:
                    project()
                if isinstance(t, int) and t == -2:
                    pe.wait_ge(wvo_in, 32)
                    pe.transpose(pv[:, 0:DK], w_rows[0:DK, 1, :], ident32[0:DK, 0:DK]).then_inc(s_wt, 1)
                    pe.transpose(ffn_bank[0][0:DK, 0:P], w_rows[:, 2, 0:DK], ident32).then_inc(s_wt, 1)
                    pe.wait_ge(s_wvo_copied, 2)
                ex(1)
                if prep:
                    score_maxima(n, npar, 0)
                if attn:
                    weigh_values(t, par, 2)
                ex(2)
                if prep:
                    score_maxima(n, npar, 1)
                if attn:
                    weigh_values(t, par, 3)
                ex(3)
                if prep:
                    score_maxima(n, npar, 2)
                if attn:
                    if proj and not first:
                        wait_alone(pe, (o_ready, t + 1), (qk_scaled, t + 3))
                    else:
                        wait_alone(pe, (o_ready, t + 1))
                        if prep:
                            pe.wait_ge(v_copied, n + 1)
                        else:
                            pe.wait_ge(logits_read, t)
                    for w in range(NWIN):
                        mm = pe.transpose(misc[0:DK, w * W:(w + 1) * W],
                                          o_norm[:, w * H:(w + 1) * H, :].rearrange("p h d -> p (h d)"),
                                          const[:, C_IDENT:C_IDENT + P])
                    mm.then_inc(o_t, 1)
                if prep:
                    score_maxima(n, npar, 3)
                ex(4, range(KC // 2))
                if attn:
                    pe.wait_ge(gelu_done, t + 1)
                    pe.matmul(misc[:, :], wo_t[:, :], o_gelu[:, :], start=True, stop=True).then_inc(wo_done, 1)
                if first:
                    pe.wait_ge(attn_masked, 1)
                    project()
                ex(4, range(KC // 2, KC))
                if prep:
                    pe.wait_ge(shifts_ready, n + 1)
                    wait(pe, pv_read, 2 * n)
                    for i in range(NG * NWIN):
                        mm = pe.transpose(pv16[AUX:ROWS_ALL, i * W:(i + 1) * W], shifts[:, i, :], ident16[:, :])
                    mm.then_inc(shifts_t, 1)
                ex(5)
                if attn:
                    if first:
                        pe.wait_ge(qk_scaled, 3)
                    pe.wait_ge(xn2_ready, t + 1)
                    for c in range(KC):
                        mm = pe.transpose(misc[:, c * P:(c + 1) * P], xn2[:, c * P:(c + 1) * P],
                                          const[:, C_IDENT:C_IDENT + P])
                    mm.then_inc(xn2_t, 1)

            steps(pe, step)

        @block.scalar
        def _(act):
            act.sem_inc(relu_done, START)
            act.wait_ge(s_init, 6)

            def expert_sum(e):
                act.wait_ge(we_loaded[e % WE_BUFS], 16 * (e // WE_BUFS + 1))
                if e > WE_BUFS:
                    act.wait_ge(s_sum, e)
                act.activation(we_lo[:, min(e, WE_BUFS), :, :].rearrange(flat), we_buf(e), ACT.Abs,
                               accum_out=we_bound[:, e:e + 1]).then_inc(s_sum, 1)

            def bias_of_experts(b, end):
                act.wait_ge(bias_in, 16)
                for e in range(b, end):
                    act.wait_ge(s_wscale, 5 * e + 5)
                    act.activation(expert_bias[:, e, :], expert_bias[:, e, :], ACT.Copy,
                                   scale=we_scale[:, e:e + 1]).then_inc(s_ebias, 1)

            def step(t, par, late=False, ffn=False, attn=False, prep=False, proj=False):
                n, npar = t + 1, (par + 1) % 2
                f, fpar = t - 1, (par + 1) % 2
                m = t + 2
                pre, start, first, second = (isinstance(t, int) and t == at for at in (-2, -1, 0, 1))

                def relu(e, fb=f, half=fpar, on=ffn):
                    if not on:
                        return
                    act.wait_ge(biased, E * fb + e + 1)
                    if e == 0:
                        act.wait_ge(gates_ready, fb + 1)
                        act.wait_ge(out_done[half], 16 * START + 8 * (fb - half))
                        to = total[:, half, :]
                    else:
                        act.wait_ge(summed, START + (E - 1) * fb + max(e - 2, 0))
                        to = expert_out[:, e % 2, :]
                    act.activation(to, ffn_bank[e % 2][:, :], ACT.Relu, scale=gate[:, half, e:e + 1]).then_inc(relu_done, 1)

                def normalize(b):
                    act.wait_ge(s_shift1, min(b + 1, 3) if isinstance(b, int) else 3)
                    wait(act, qk_proj, b)
                    act.activation(xn[:, :], x_all[:, b, :], ACT.Identity, bias=shift1[:, b, :],
                                   scale=rstd1[:, b, 1:2]).then_inc(xn_ready, 1)

                def exp(w):
                    if not attn:
                        return
                    act.wait_ge(scores_t, NWIN * t + w + 1)
                    wait(act, lo_done, NWIN * t + w - 1)
                    wait(act, pv_done, NWIN * t + w - 1)
                    act.activation(prob_hi[:, w % 2, :], score[w % 2][:, :], ACT.Exp, scale=exp_scale).then_inc(hi_done, 1)
                    act.activation(prob32[:, w % 2, :], score[w % 2][:, :], ACT.Exp, scale=exp_scale).then_inc(exp_done, 1)

                def scale_projection():
                    act.wait_ge(qk_proj, m + 1)
                    wait(act, lo_ready, m)
                    if pre:
                        act.wait_ge(s_scale, 2)
                    act.activation(qk32[:, :], misc[:, :], ACT.Identity, bias=bias_qk, scale=scale_qk).then_inc(qk_scaled, 1)

                def high_projection():
                    act.wait_ge(k_masked, m + 1)
                    wait(act, stacks_in, 16 * STACK_DMAS * m)
                    act.activation(qk_hi[:, :], qk32[:, :], ACT.Copy).then_inc(hi_ready, 1)

                relu(E - 2, t - 2, par, late)
                if pre:
                    normalize(0)
                exp(0)
                exp(1)
                relu(E - 1, t - 2, par, late)
                if prep:
                    act.wait_ge(v_proj, n + 1)
                    wait(act, v_ready, n)
                    act.activation(v32[:, :, :].rearrange("p x d -> p (x d)"), misc[:, 0:NWIN * DK],
                                   ACT.Copy).then_inc(v_copied, 1)
                if proj and not (pre or first):
                    normalize(m)
                exp(2)
                relu(0)
                if proj and not first:
                    scale_projection()
                exp(3)
                if first:
                    expert_sum(4)
                    expert_sum(5)
                if proj and not first:
                    high_projection()
                if pre:
                    act.wait_ge(s_wt, 2)
                    act.activation(wv_t[:, :], pv[:, 0:DK], ACT.Copy).then_inc(s_wvo_copied, 1)
                    act.wait_ge(small_in, 16 * 6)
                    act.activation(tg, g2, ACT.Tanh).then_inc(s_tanh, 1)
                    act.wait_ge(s_tanh, 1)
                    act.wait_ge(s_wt, 3)
                    act.activation(wo_t[:, :], ffn_bank[0][0:DK, 0:P], ACT.Copy, scale=tg[0:DK, 0:1]).then_inc(s_wvo_copied, 1)
                relu(1)
                if attn:
                    act.activation(table[:, 2:3], table[:, 1:2], ACT.Gelu)
                if first:
                    bias_of_experts(0, 3)
                if second:
                    bias_of_experts(3, E)
                relu(2)
                if start:
                    for e in range(4):
                        expert_sum(e)
                if attn:
                    act.wait_ge(o_t, t + 1)
                    wait(act, wo_done, t)
                    if first:
                        act.wait_ge(small_in, 16 * 6)
                    act.activation(o_gelu[:, :], misc[0:DK, :], ACT.Gelu, bias=bv_c[0:DK, :]).then_inc(gelu_done, 1)
                    if first:
                        normalize(2)
                    act.activation(table[:, 0:1], table[:, 1:2], ACT.Exp)
                relu(3)
                relu(4)
                if first:
                    expert_sum(6)
                    scale_projection()
                if prep:
                    act.wait_ge(shifts_t, n + 1)
                    if start:
                        act.wait_ge(s_init, 5)
                    act.activation(q_stack[AUX:ROWS_ALL, npar, :, :].rearrange("p g s -> p (g s)"),
                                   pv16[AUX:ROWS_ALL, :], ACT.Copy).then_inc(shift_rows, 1)
                if attn:
                    act.wait_ge(xn2_t, t + 1)
                    wait(act, ffn_done, START + E * (t - 1))
                    act.activation(xt_hi[:, par, :, :].rearrange("p c t -> p (c t)"), misc[:, :],
                                   ACT.Copy).then_inc(xt_hi_ready, 1)
                if first:
                    high_projection()
                    expert_sum(7)
                relu(5)

            steps(act, step)

        @block.vector
        def _(dve):
            def shift_of_norm(b, e):
                dve.scalar_tensor_tensor(shift1[:, b:e, 0], mean_var1[:, b:e, 0], -1.0, rstd1[:, b:e, 1],
                                         ALU.mult, ALU.mult).then_inc(s_shift1, 1)

            dve.memset(half_neg[:, :], -0.5).then_inc(s_init, 1)
            dve.memset(table[:, :], 0.0).then_inc(s_init, 1)
            dve.memset(q_stack[AUX:P, :, :, :], MASK_Q).then_inc(s_init, 1)
            dve.memset(shifts[:, :, 0:1], MASK_Q).then_inc(s_init, 1)
            dve.memset(v_thirds[:, :, :, :, DH:VC], 0.0).then_inc(s_init, 1)
            dve.wait_ge(s_init, 5)
            dve.memset(v_thirds[:, :, :, 0, DH:VC], 1.0).then_inc(s_init, 1)
            dve.wait_ge(x0_in, 16)
            dve.bn_stats(stats1[:, 0, :], x_all[:, 0, :]).then_inc(s_stat, 1)
            dve.wait_ge(s_stat, 1)
            dve.bn_aggr(mean_var1[:, 0, :], stats1[:, 0, :]).then_inc(s_stat, 1)
            dve.wait_ge(s_stat, 2)
            dve.tensor_scalar(rstd1[:, 0, 0:1], mean_var1[:, 0, 1:2], EPS, None, ALU.add).then_inc(s_var1, 1)
            dve.wait_ge(s_wt, 1)
            dve.tensor_copy(wqk_t[:, :], misc[:, 0:P]).then_inc(s_wqk_copied, 1)
            dve.wait_ge(const_in, 16)
            dve.wait_ge(s_rstd1, 1)
            shift_of_norm(0, 1)
            dve.wait_ge(wqk_in, 32)
            dve.tensor_reduce(qk_small[:, 0:1], w_rows[:, 0, :], AX.X, ALU.add, apply_absolute_value=True).then_inc(s_sums, 1)
            dve.wait_ge(bqk_in, 32)
            dve.tensor_reduce(qk_small[:, 1:2], bqk, AX.X, ALU.max, apply_absolute_value=True).then_inc(s_sums, 1)
            dve.wait_ge(s_sums, 2)
            dve.tensor_scalar(bound, qk_small[:, 0:1], NORM_BOUND, qk_small[:, 1:2], ALU.mult, ALU.add).then_inc(s_sums, 1)
            dve.wait_ge(s_sums, 3)
            dve.tensor_scalar(qk_small[:, 2:4], const[:, C_SIDE:C_SIDE + 2], bound, QK_FLOOR, ALU.mult, ALU.max).then_inc(s_sums, 1)
            dve.wait_ge(s_bound, 1)
            dve.tensor_scalar(qk_small[:, 4:6].bitcast(I32), qk_small[:, 4:6].bitcast(I32), 0x7F800000, None,
                              ALU.bitwise_and).then_inc(s_sums, 1)
            dve.wait_ge(s_sums, 5)
            dve.reciprocal(qk_small[:, 6:8], qk_small[:, 4:6]).then_inc(s_sums, 1)
            dve.tensor_scalar(exp_scale, qk_small[:, 4:5], qk_small[:, 5:6], float(DH) ** -0.5 / QK_TOP ** 2,
                              ALU.mult, ALU.mult).then_inc(s_sums, 1)
            dve.wait_ge(s_sums, 7)
            dve.tensor_scalar(scale_qk[0:DK, :], qk_small[0:DK, 6:7], QK_TOP, None, ALU.mult).then_inc(s_sums, 1)
            dve.tensor_scalar(scale_qk[DK:2 * DK, :], qk_small[DK:2 * DK, 7:8], QK_TOP, None, ALU.mult).then_inc(s_scale, 1)
            dve.wait_ge(s_sums, 8)
            dve.wait_ge(s_scale, 1)
            dve.tensor_tensor(bias_qk, bqk, scale_qk, ALU.mult).then_inc(s_scale, 1)

            def statistics(b, e):
                dve.wait_ge(x1_in if b == 1 else xrest_in, 16)
                for i in range(b, e):
                    dve.bn_stats(stats1[:, i, :], x_all[:, i, :]).then_inc(s_stat, 1)
                for i in range(b, e):
                    dve.wait_ge(s_stat, b + i + 1)
                    dve.bn_aggr(mean_var1[:, i, :], stats1[:, i, :]).then_inc(s_stat, 1)
                dve.wait_ge(s_stat, 2 * e)
                dve.tensor_scalar(rstd1[:, b:e, 0], mean_var1[:, b:e, 1], EPS, None, ALU.add).then_inc(s_var1, 1)

            def expert_scale(e):
                one = slice(e, e + 1)
                dve.wait_ge(s_sum_all, e + 1)
                dve.tensor_scalar(we_pow[:, one], we_bound_all[:, one], 2.0 ** -100, None, ALU.max).then_inc(s_wscale, 1)
                dve.wait_ge(s_wscale, 5 * e + 1)
                dve.tensor_scalar(we_pow[:, one].bitcast(I32), we_pow[:, one].bitcast(I32), 0x7F800000, None,
                                  ALU.bitwise_and).then_inc(s_wscale, 1)
                dve.wait_ge(s_wscale, 5 * e + 2)
                dve.reciprocal(we_scale[:, one], we_pow[:, one]).then_inc(s_wscale, 1)
                dve.tensor_scalar(we_unscale[:, one], we_pow[:, one], 0.5 / WE_TOP, None, ALU.mult).then_inc(s_wscale, 1)
                dve.wait_ge(s_wscale, 5 * e + 3)
                dve.tensor_scalar(we_scale[:, one], we_scale[:, one], WE_TOP, None, ALU.mult).then_inc(s_wscale, 1)

            def expert_low(e):
                dve.wait_ge(s_whi, e + 1)
                if e >= E - 2:
                    wait_low(dve, WE_BUFS - 1)
                dve.scalar_tensor_tensor(we_lo[:, e, :, :].rearrange(flat), we_buf(e), we_scale[:, e:e + 1],
                                         we_hi[:, e, :, :].rearrange(flat), ALU.mult, ALU.subtract).then_inc(dve_low, 1)

            def step(t, par, late=False, ffn=False, attn=False, prep=False, proj=False):
                n, npar = t + 1, (par + 1) % 2
                f, fpar = t - 1, (par + 1) % 2
                m = t + 2
                pre, start, first, second = (isinstance(t, int) and t == at for at in (-2, -1, 0, 1))

                def add_bias(e, fb=f, on=ffn):
                    if not on:
                        return
                    dve.wait_ge(ffn_done, START + E * fb + e + 1)
                    if isinstance(t, int) and t == 1:
                        dve.wait_ge(s_ebias, e + 1)
                    dve.tensor_tensor(ffn_bank[e % 2][:, :], ffn_bank[e % 2][:, :], expert_bias[:, e, :],
                                      ALU.add).then_inc(biased, 1)

                def low_half(w):
                    if not attn:
                        return
                    dve.wait_ge(exp_done, NWIN * t + w + 1)
                    wait(dve, pv_done, NWIN * t + w - 1)
                    dve.tensor_tensor(prob_lo[:, w % 2, :], prob32[:, w % 2, :], prob_hi[:, w % 2, :],
                                      ALU.subtract).then_inc(lo_done, 1)

                def maxima(w):
                    if not prep:
                        return
                    dve.wait_ge(scores, NWIN * n + w + 1)
                    dve.tensor_reduce(row_max[:, :, w, :], score[w % 2][:, :].rearrange("p (g h j) -> p g h j", g=NG, h=HG),
                                      AX.X, ALU.max).then_inc(max_done, 1)

                def add_windows(half):
                    if not attn:
                        return
                    dve.wait_ge(pv_done, NWIN * t + 2 * half + 2)
                    n_in = 2 * H
                    dve.tensor_reduce(o_sum[:, half * n_in:(half + 1) * n_in, :],
                                      pv[:, 0:n_in * THIRDS * VC].rearrange("p (x q c) -> p x c q", q=THIRDS, c=VC),
                                      AX.X, ALU.add).then_inc(pv_read, 1)

                if pre:
                    dve.wait_ge(mask_early_in, 16)

                def make_stack():
                    if not prep:
                        return
                    dve.wait_ge(stacks_in, 16 * STACK_DMAS * (n + 1))
                    dve.wait_ge(mask_row, n + 1)
                    wait(dve, scores_t, NWIN * (n - 1))
                    for h in range(HG):
                        mm = dve.tensor_scalar(k_stack[:, npar, :, h, :], k_rows[:, :, :], const[:, C_HEAD + h:C_HEAD + h + 1],
                                               const[:, C_ONE + h:C_ONE + h + 1], ALU.mult, ALU.add)
                    mm.then_inc(k_ready, 1)

                def mask_keys():
                    dve.wait_ge(qk_scaled, m + 1)
                    dve.scalar_tensor_tensor(qk32[DK:2 * DK, :], mask_all[DK:2 * DK, m, :], 0.0, qk32[DK:2 * DK, :],
                                             ALU.is_gt, ALU.mult).then_inc(k_masked, 1)

                def low_projection():
                    dve.wait_ge(hi_ready, m + 1)
                    wait(dve, stacks_in, 16 * STACK_DMAS * m)
                    dve.tensor_tensor(qk_lo[:, :], qk32[:, :], qk_hi[:, :], ALU.subtract).then_inc(lo_ready, 1)

                def row_of_mask():
                    if not isinstance(t, int):
                        dve.wait_ge(mask_in, 16)
                    wait(dve, k_ready, m)
                    dve.tensor_scalar(k_rows[AUX:P, :, :], mask_all[AUX:P, m, :].unsqueeze(1).broadcast_to([P - AUX, NG, S]),
                                      0.0, -AUX_K, ALU.is_le, ALU.mult).then_inc(mask_row, 1)

                if start:
                    mask_keys()
                    statistics(2, B)
                if late:
                    add_bias(E - 2, t - 2, late)
                if ffn:
                    dve.wait_ge(logits, f + 1)
                    dve.tensor_reduce(logit[:, 0, :], misc[:, 0:THIRDS * E].rearrange("p (q e) -> p e q", q=THIRDS),
                                      AX.X, ALU.add).then_inc(logits_read, 1)
                    dve.wait_ge(logits_read, f + 1)
                    dve.tensor_tensor(logit[:, 1, :], logit[:, 0, :], bg_b[:, :], ALU.add).then_inc(s_gate, 1)
                    dve.wait_ge(s_gate, 7 * f + 1)
                    other = logit[:, 1, :].unsqueeze(1).broadcast_to([P, E, E])
                    own = logit[:, 1, :].unsqueeze(2).broadcast_to([P, E, E])
                    earlier = const[:, C_EARLIER:C_EARLIER + E * E].rearrange("p (e j) -> p e j", e=E)
                    dve.tensor_tensor(pairs[:, 0, :, :], other, own, ALU.is_gt).then_inc(s_gate, 1)
                    dve.tensor_tensor(pairs[:, 1, :, :], other, own, ALU.is_equal).then_inc(s_gate, 1)
                    dve.wait_ge(s_gate, 7 * f + 3)
                    dve.tensor_tensor(pairs[:, 1, :, :], pairs[:, 1, :, :], earlier, ALU.mult).then_inc(s_gate, 1)
                    dve.tensor_reduce(rank[:, 0, :], pairs[:, 0, :, :], AX.X, ALU.add).then_inc(s_gate, 1)
                    dve.wait_ge(s_gate, 7 * f + 4)
                    dve.tensor_reduce(rank[:, 1, :], pairs[:, 1, :, :], AX.X, ALU.add).then_inc(s_gate, 1)
                    dve.wait_ge(s_gate, 7 * f + 6)
                    dve.tensor_tensor(rank[:, 0, :], rank[:, 0, :], rank[:, 1, :], ALU.add).then_inc(s_gate, 1)
                    dve.wait_ge(s_gate, 7 * f + 7)
                    wait(dve, relu_done, START + E * (f - 1))
                    dve.scalar_tensor_tensor(gate[:, fpar, :], rank[:, 0, :], 1.5, we_unscale[:, :], ALU.is_lt,
                                             ALU.mult).then_inc(gates_ready, 1)
                if start or first:
                    make_stack()
                low_half(0)
                if late:
                    add_bias(E - 1, t - 2, late)
                low_half(1)
                if first:
                    expert_low(2)
                    expert_scale(3)
                if not (start or first):
                    make_stack()
                add_bias(0)
                if proj:
                    row_of_mask()
                low_half(2)
                if proj and not (start or first):
                    mask_keys()
                if attn:
                    add_windows(0)
                if late:
                    dve.wait_ge(summed, START + (E - 1) * (t - 1))
                    dve.scalar_tensor_tensor(total[:, par, :], total[:, par, :], tg[:, 1:2], x_all[:, t - 2, :],
                                             ALU.mult, ALU.add).then_inc(out_ready, 1)
                add_bias(1)
                if second:
                    expert_low(4)
                if proj and not first:
                    low_projection()
                if pre:
                    dve.tensor_copy(ident16[:, :], const[:, C_IDENT:C_IDENT + P]).then_inc(s_init, 1)
                    statistics(1, 2)
                    dve.wait_ge(s_rstd1, 2)
                    shift_of_norm(1, 2)
                    dve.wait_ge(s_tanh, 1)
                    dve.tensor_tensor(bo_c, bo_c, tg[:, 0:1], ALU.mult).then_inc(s_wot, 1)
                    dve.tensor_copy(wg_thirds[:, :, 0, :], wg_in[:, :, :]).then_inc(s_wg, 1)
                    dve.wait_ge(s_wg, 1)
                    dve.tensor_tensor(wg_rest[:, :, :], wg_in[:, :, :], wg_thirds[:, :, 0, :], ALU.subtract).then_inc(s_wg, 1)
                    dve.wait_ge(s_wg, 2)
                    dve.tensor_copy(wg_thirds[:, :, 1, :], wg_rest[:, :, :]).then_inc(s_wg, 1)
                    dve.wait_ge(s_wg, 3)
                    dve.tensor_tensor(wg_thirds[:, :, 2, :], wg_rest[:, :, :], wg_thirds[:, :, 1, :], ALU.subtract).then_inc(s_wg, 1)

                low_half(3)
                maxima(0)
                if start:
                    expert_scale(0)
                add_bias(2)
                maxima(1)
                if attn:
                    add_windows(1)
                    dve.wait_ge(pv_read, 2 * t + 2)
                    dve.reciprocal(o_den[:, :], o_sum[:, :, DH]).then_inc(den_ready, 1)
                    dve.wait_ge(den_ready, t + 1)
                    wait(dve, o_t, t)
                    dve.tensor_tensor(o_norm[:, :, :], o_sum[:, :, 0:DH],
                                      o_den[:, :].unsqueeze(2).broadcast_to([P, NWIN * H, DH]), ALU.mult).then_inc(o_ready, 1)
                add_bias(3)
                maxima(2)
                if start:
                    expert_scale(1)
                maxima(3)
                if prep:
                    dve.wait_ge(max_done, NWIN * (n + 1))
                    wait(dve, shifts_t, n)
                    rows = row_max[:, :, :, :].rearrange("p g w h -> p (g w) h")
                    dve.tensor_scalar(shifts[:, :, 1:1 + HG], rows, -1.0 / AUX_K, None, ALU.mult).then_inc(max_hi, 1)
                    dve.wait_ge(max_hi, n + 1)
                    dve.scalar_tensor_tensor(shifts[:, :, 1 + HG:1 + 2 * HG], rows, -1.0 / AUX_K, shifts[:, :, 1:1 + HG],
                                             ALU.mult, ALU.subtract).then_inc(shifts_ready, 1)
                if start:
                    dve.wait_ge(s_rstd1, 3)
                    shift_of_norm(2, B)
                    expert_low(0)
                    expert_scale(2)
                if not attn:
                    add_bias(4)
                if attn:
                    dve.wait_ge(wo_done, t + 1)
                    if first:
                        dve.wait_ge(s_wot, 1)
                    dve.scalar_tensor_tensor(attn_out[:, :], misc[:, :], bo_c, mask_all[:, t, :], ALU.add,
                                             ALU.mult).then_inc(attn_masked, 1)
                    dve.wait_ge(attn_masked, t + 1)
                    dve.tensor_tensor(x_all[:, t, :], x_all[:, t, :], attn_out[:, :], ALU.add).then_inc(x1_ready, 1)
                    wait_alone(dve, (x1_ready, t + 1))
                    dve.bn_stats(stats2[:, :], x_all[:, t, :]).then_inc(s_stat2, 1)
                    wait_alone(dve, (s_stat2, 2 * t + 1))
                    dve.bn_aggr(mean_var2[:, 0:2], stats2[:, :]).then_inc(s_stat2, 1)
                    dve.wait_ge(s_stat2, 2 * t + 2)
                    dve.tensor_scalar(mean_var2[:, 2:3], mean_var2[:, 1:2], EPS, None, ALU.add).then_inc(s_var2, 1)
                    if first:
                        expert_scale(4)
                        expert_scale(5)
                    add_bias(4)
                    dve.wait_ge(s_rstd2, t + 1)
                    wait(dve, xn2_t, t)
                    dve.tensor_scalar(xn2[:, :], x_all[:, t, :], mean_var2[:, 0:1], mean_var2[:, 3:4],
                                      ALU.subtract, ALU.mult).then_inc(xn2_ready, 1)
                if second:
                    expert_low(6)
                add_bias(5)
                if first:
                    mask_keys()
                if attn:
                    dve.wait_ge(xt_hi_ready, t + 1)
                    dve.tensor_tensor(xt_lo[:, par, :, :].rearrange("p c t -> p (c t)"), misc[:, :],
                                      xt_hi[:, par, :, :].rearrange("p c t -> p (c t)"), ALU.subtract).then_inc(xt_lo_ready, 1)
                if first:
                    low_projection()
                    expert_low(3)
                    expert_scale(6)
                    expert_scale(7)

            steps(dve, step)

        @block.gpsimd
        def _(pool):
            def load_expert(e):
                pool.dma_start(we_buf(e).rearrange("p (k s) -> p k s", k=KC),
                               w_e[e].rearrange("(k p) s -> p k s", p=P)).then_inc(we_loaded[e % WE_BUFS], 16)

            def expert_bound(e):
                pool.wait_ge(s_sum, e + 1)
                pool.partition_all_reduce(we_bound_all[:, e:e + 1], we_bound[:, e:e + 1], P, MAXIMUM).then_inc(s_sum_all, 1)

            def expert_hi(e):
                pool.wait_ge(s_wscale, 5 * e + 5)
                if e >= E - 2:
                    wait_low(pool, WE_BUFS - 2)
                pool.tensor_scalar(we_hi[:, e, :, :].rearrange(flat), we_buf(e),
                                   we_scale[:, e:e + 1], 1.0, ALU.mult, ALU.mult).then_inc(s_whi, 1)

            def expert_low(e):
                pool.tensor_scalar(we_buf(e), we_buf(e), we_scale[:, e:e + 1], 1.0, ALU.mult, ALU.mult).then_inc(s_wscaled, 1)
                pool.wait_ge(s_wscaled, low_of_pool.index(e) + 1)
                pool.wait_ge(s_whi, e + 1)
                if e >= E - 2:
                    wait_low(pool, WE_BUFS - 1)
                pool.tensor_tensor(we_lo[:, e, :, :].rearrange(flat), we_buf(e), we_hi[:, e, :, :].rearrange(flat),
                                   ALU.subtract).then_inc(pool_low, 1)

            pool.sem_inc(summed, START)
            pool.wait_ge(s_init, 1)

            def rstd_of(b, e):
                pool.wait_ge(s_var1, min(b, 2) + 1)
                pool.tensor_tensor(rstd1[:, b:e, 1], rstd1[:, b:e, 0], half_neg[:, :].broadcast_to([P, e - b]),
                                   ALU.pow).then_inc(s_rstd1, 1)

            rstd_of(0, 1)
            pool.wait_ge(s_sums, 4)
            pool.partition_all_reduce(qk_small[:, 4:6], qk_small[:, 2:4], P, MAXIMUM).then_inc(s_bound, 1)
            pool.wait_ge(wvo_in, 32)
            load_expert(0)

            def step(t, par, late=False, ffn=False, attn=False, prep=False, proj=False):
                n, npar = t + 1, (par + 1) % 2
                f, fpar = t - 1, (par + 1) % 2
                pre, start, first, second = (isinstance(t, int) and t == at for at in (-2, -1, 0, 1))

                def accumulate(e, fb=f, half=fpar, on=ffn):
                    if not on:
                        return
                    pool.wait_ge(relu_done, START + E * fb + e + 1)
                    pool.wait_ge(summed, START + (E - 1) * fb + e - 1)
                    pool.tensor_tensor(total[:, half, :], total[:, half, :], expert_out[:, e % 2, :],
                                       ALU.add).then_inc(summed, 1)

                def rstd_of_second():
                    pool.wait_ge(s_var2, t + 1)
                    pool.tensor_tensor(mean_var2[:, 3:4], mean_var2[:, 2:3], half_neg[:, :], ALU.pow).then_inc(s_rstd2, 1)

                if late:
                    accumulate(E - 2, t - 2, par, late)
                    accumulate(E - 1, t - 2, par, late)
                if pre:
                    rstd_of(1, 2)
                if prep:
                    thirds = v_thirds[:, npar, :, :, :]
                    wait_alone(pool, (v_copied, n + 1), (pv_done, NWIN * (n - 1)))
                    if isinstance(n, int) and n == 0:
                        pool.wait_ge(s_init, 6)
                    pool.tensor_copy(thirds[:, :, 0, 0:DH], v32[:, :, :]).then_inc(v_step, 1)
                    pool.wait_ge(v_step, 4 * n + 1)
                    pool.tensor_tensor(v32[:, :, :], v32[:, :, :], thirds[:, :, 0, 0:DH], ALU.subtract).then_inc(v_step, 1)
                    wait_alone(pool, (v_step, 4 * n + 2))
                    pool.tensor_copy(thirds[:, :, 1, 0:DH], v32[:, :, :]).then_inc(v_step, 1)
                    pool.wait_ge(v_step, 4 * n + 3)
                    pool.tensor_tensor(v32[:, :, :], v32[:, :, :], thirds[:, :, 1, 0:DH], ALU.subtract).then_inc(v_step, 1)
                    wait_alone(pool, (v_step, 4 * n + 4))
                    pool.tensor_copy(thirds[:, :, 2, 0:DH], v32[:, :, :]).then_inc(v_ready, 1)
                if start:
                    load_expert(1)
                    load_expert(2)
                    rstd_of(2, B)
                    load_expert(3)
                    expert_bound(0)
                    expert_bound(1)
                    expert_hi(0)
                    load_expert(4)
                    expert_bound(2)
                    expert_hi(1)
                    expert_bound(3)
                    wait_low(pool, 0)
                    load_expert(5)
                    expert_hi(2)
                    expert_low(1)
                    wait_low(pool, 1)
                    load_expert(6)
                    wait_low(pool, 2)
                    load_expert(7)
                    expert_hi(3)
                if first:
                    expert_bound(4)
                    expert_bound(5)
                    rstd_of_second()
                    expert_hi(4)
                    expert_bound(6)
                    expert_bound(7)
                    expert_hi(5)
                    expert_hi(6)
                    expert_hi(7)
                if second:
                    expert_low(5)
                accumulate(1)
                if second:
                    expert_low(E - 1)
                accumulate(2)
                accumulate(3)
                if attn and not first:
                    rstd_of_second()
                accumulate(4)
                accumulate(5)

            steps(pool, step)


_INS = ["x", "ctx_4096", "mask_Bx1x4096_ff1", "g_xattn", "g_ffn", "L0_xattn_Wq", "L0_xattn_bq", "L0_xattn_Wk",
        "L0_xattn_bk", "L0_xattn_Wv", "L0_xattn_bv", "L0_xattn_Wo", "L0_xattn_bo", "L0_ffn_W_gate",
        "L0_ffn_b_gate", "L0_ffn_W_e", "L0_ffn_b_e"]


def kernel(**inputs):
    import numpy as np
    import concourse.bacc as bacc
    from concourse.bass_utils import run_bass_kernel_spmd as run

    nc = bacc.Bacc("TRN2", target_bir_lowering=False, num_devices=1)
    arrays, args = {}, []
    for name in _INS:
        a = np.ascontiguousarray(inputs[name])
        arrays[f"in_{name}"] = a
        args.append(nc.dram_tensor(f"in_{name}", a.shape, mybir.dt.from_np(a.dtype), kind="ExternalInput").ap())
    arrays["in_constants"] = shape_constants()
    args.append(nc.dram_tensor("in_constants", (P, C_END), F32, kind="ExternalInput").ap())
    args.append(nc.dram_tensor("out_0", (B, D, S), F32, kind="ExternalOutput").ap())
    build(nc, *args)
    return run(nc, [arrays], core_ids=[0]).results[0]["out_0"]
```
